# Optimizing a Trainium2 kernel written in Bass

```python
import numpy as np
import jax
import jax.numpy as jnp

def _softmax(x, axis=-1):
    return jax.nn.softmax(x, axis=axis)

def _gelu(x):
    return jax.nn.gelu(x, approximate=True)

def _silu(x):
    return jax.nn.silu(x)

def _sigmoid(x):
    return jax.nn.sigmoid(x)

def _layernorm(x, axis=-1, eps=1e-05):
    m = jnp.mean(x, axis=axis, keepdims=True)
    v = jnp.var(x, axis=axis, keepdims=True)
    return (x - m) / jnp.sqrt(v + eps)

def _scatter_add(tgt, idx, src, axis=0):
    return tgt.at[idx].add(src)

def _segment_sum(src, seg, n):
    return jax.ops.segment_sum(src, seg, n)
kernel_name = 'mk_flamingo_gated_d1_seqx_r4_1890fa'

def setup_inputs(seed: int=0):
    np.random.seed(seed)
    _w = jnp.asarray

    def _rec_inputs():
        import jax
        import jax.numpy as jnp
        _rk = jax.random.key(seed)
        x = 0.0003765 + 1 * jax.random.normal(jax.random.fold_in(_rk, 1), (16, 256, 512), jnp.float32)
        _lenS = 256 - jax.random.randint(jax.random.fold_in(_rk, 7), (16,), 0, max(1, 256 // 4) + 1, jnp.int32)
        _lenS2 = 256 - jax.random.randint(jax.random.fold_in(_rk, 8), (16,), 0, max(1, 256 // 4) + 1, jnp.int32)
        _ctx_2048P = jax.random.normal(jax.random.fold_in(_rk, 11), (16, 16, 512), jnp.float32)
        _ctx_2048c = jax.random.dirichlet(jax.random.fold_in(_rk, 511), 0.3 * jnp.ones((16,), jnp.float32), (16, 256))
        _ctx_2048t = jnp.einsum('bsk,bkd->bsd', _ctx_2048c, _ctx_2048P)
        _ctx_2048t = _ctx_2048t * jax.lax.rsqrt(jnp.mean(jnp.square(_ctx_2048t)) + 1e-12) * 0.953939
        ctx_2048 = -0.000292821 + 1.00034 * (_ctx_2048t + 0.3 * jax.random.normal(jax.random.fold_in(_rk, 611), (16, 256, 512), jnp.float32))
        _g = jax.random.normal(jax.random.fold_in(_rk, 9001), (2, 1), jnp.float32)
        _g = jnp.sign(_g) * jnp.maximum(jnp.abs(_g), 1.0) + (_g == 0) * 1.0
        g_xattn = _g[0]
        g_ffn = _g[1]
        return (x, ctx_2048, g_xattn, g_ffn)
    x, ctx_2048, g_xattn, g_ffn = _rec_inputs()

    def _L0_xattn_setup():
        import jax, jax.numpy as jnp
        import numpy as np
        key = jax.random.key(seed)
        k1, k2, k3, k4, k5 = jax.random.split(key, 5)
        B, D_MODEL, L = (2, 256, 512)
        HEAD_DIM = 8
        H = D_MODEL // HEAD_DIM
        return {'k': jax.random.normal(k1, (B, D_MODEL, L), dtype=jnp.float32), 'v': jax.random.normal(k2, (B, D_MODEL, L), dtype=jnp.float32), 'q': jax.random.normal(k3, (B, D_MODEL, L), dtype=jnp.float32), 'ssm_kernel': jax.random.normal(k4, (H, L), dtype=jnp.float32), 'D': jax.random.normal(k5, (H,), dtype=jnp.float32), 'head_dim': HEAD_DIM}
    _L0_xattn_all = _L0_xattn_setup()
    _L0_xattn_in = {k: v for k, v in _L0_xattn_all.items() if k in ('ssm_kernel', 'D')}
    del _L0_xattn_all

    def _L0_ffn_setup():
        import jax, jax.numpy as jnp
        import numpy as np
        _FP4_LUT = jnp.array([0.0, 0.5, 1.0, 1.5, 2.0, 3.0, 4.0, 6.0, -0.0, -0.5, -1.0, -1.5, -2.0, -3.0, -4.0, -6.0], dtype=jnp.float32)
        GROUP_SIZE = 128
        EPS = 1e-06

        def _dequant_fp4(packed_i32, scales_f16, group_size):
            out_f, in_p = packed_i32.shape
            w = packed_i32.astype(jnp.uint32)
            shifts = jnp.arange(8, dtype=jnp.uint32) * 4
            nib = w[:, :, None] >> shifts & jnp.uint32(15)
            vals = _FP4_LUT[nib.astype(jnp.int32)].reshape(out_f, in_p * 8)
            s = scales_f16.astype(jnp.float32).T
            s_full = jnp.repeat(s, group_size, axis=1)
            return vals * s_full
        key = jax.random.key(seed)
        k1, k2, k3, k4, k5 = jax.random.split(key, 5)
        B, S, H, I = (4, 512, 512, 1408)
        x = jax.random.normal(k1, (B, S, H), dtype=jnp.float32)
        gate_up_packed = jax.random.randint(k2, (2 * I, H // 8), 0, 2147483647, dtype=jnp.int32)
        gate_up_scales = jax.random.uniform(k3, (H // GROUP_SIZE, 2 * I), dtype=jnp.float32).astype(jnp.float16)
        down_packed = jax.random.randint(k4, (H, I // 8), 0, 2147483647, dtype=jnp.int32)
        down_scales = jax.random.uniform(k5, (I // GROUP_SIZE, H), dtype=jnp.float32).astype(jnp.float16)
        return {'x': x, 'gate_up_packed': gate_up_packed, 'gate_up_scales': gate_up_scales, 'down_packed': down_packed, 'down_scales': down_scales}
    _L0_ffn_all = _L0_ffn_setup()
    _L0_ffn_in = {k: v for k, v in _L0_ffn_all.items() if k in ('gate_up_packed', 'gate_up_scales', 'down_packed', 'down_scales')}
    del _L0_ffn_all
    return {'x': x, 'ctx_2048': ctx_2048, 'g_xattn': g_xattn, 'g_ffn': g_ffn, 'L0_xattn_ssm_kernel': _L0_xattn_in['ssm_kernel'], 'L0_xattn_D': _L0_xattn_in['D'], 'L0_ffn_gate_up_packed': _L0_ffn_in['gate_up_packed'], 'L0_ffn_gate_up_scales': _L0_ffn_in['gate_up_scales'], 'L0_ffn_down_packed': _L0_ffn_in['down_packed'], 'L0_ffn_down_scales': _L0_ffn_in['down_scales']}

def reference(x, ctx_2048, g_xattn, g_ffn, L0_xattn_ssm_kernel, L0_xattn_D, L0_ffn_gate_up_packed, L0_ffn_gate_up_scales, L0_ffn_down_packed, L0_ffn_down_scales):
    import jax
    import jax.numpy as jnp

    def _L0_xattn_ref(k, v, q, ssm_kernel, D, head_dim):
        import jax, jax.numpy as jnp
        import numpy as np
        B, HD, L = k.shape
        H = HD // head_dim
        fft_size = 2 * L
        k_ = k.reshape(B, H, head_dim, L)
        v_ = v.reshape(B, H, head_dim, L)
        q_ = q.reshape(B, H, head_dim, L)
        kv = jnp.einsum('bhil,bhjl->bijhl', k_, v_)
        kv_f = jnp.fft.rfft(kv, n=fft_size)
        kernel_f = jnp.fft.rfft(ssm_kernel, n=fft_size)
        y = jnp.fft.irfft(kv_f * kernel_f, n=fft_size)[..., :L]
        out = y + kv * D[None, None, None, :, None]
        out = jnp.einsum('bijhl,bhil->bjhl', out, q_)
        out = jnp.transpose(out, (0, 2, 1, 3)).reshape(B, H * head_dim, L)
        return out.astype(k.dtype)

    def _L0_ffn_ref(x, gate_up_packed, gate_up_scales, down_packed, down_scales):
        import jax, jax.numpy as jnp
        import numpy as np
        _FP4_LUT = jnp.array([0.0, 0.5, 1.0, 1.5, 2.0, 3.0, 4.0, 6.0, -0.0, -0.5, -1.0, -1.5, -2.0, -3.0, -4.0, -6.0], dtype=jnp.float32)
        GROUP_SIZE = 128
        EPS = 1e-06

        def _dequant_fp4(packed_i32, scales_f16, group_size):
            out_f, in_p = packed_i32.shape
            w = packed_i32.astype(jnp.uint32)
            shifts = jnp.arange(8, dtype=jnp.uint32) * 4
            nib = w[:, :, None] >> shifts & jnp.uint32(15)
            vals = _FP4_LUT[nib.astype(jnp.int32)].reshape(out_f, in_p * 8)
            s = scales_f16.astype(jnp.float32).T
            s_full = jnp.repeat(s, group_size, axis=1)
            return vals * s_full
        I = gate_up_packed.shape[0] // 2
        w_gu = _dequant_fp4(gate_up_packed, gate_up_scales, GROUP_SIZE)
        w_down = _dequant_fp4(down_packed, down_scales, GROUP_SIZE)
        gate_up = jnp.einsum('bsh,oh->bso', x, w_gu)
        gate, up = (gate_up[..., :I], gate_up[..., I:])
        h = jax.nn.silu(gate) * up
        y = jnp.einsum('bsi,hi->bsh', h, w_down)
        rms = jnp.sqrt(jnp.mean(y * y, axis=-1, keepdims=True) + EPS)
        return y / rms
    x = x + jnp.tanh(g_xattn[0]) * _L0_xattn_ref(ctx_2048, ctx_2048, _layernorm(x, axis=-1), L0_xattn_ssm_kernel, L0_xattn_D, 8)
    x = x + jnp.tanh(g_ffn[0]) * _L0_ffn_ref(_layernorm(x, axis=-1), L0_ffn_gate_up_packed, L0_ffn_gate_up_scales, L0_ffn_down_packed, L0_ffn_down_scales)
    return x

_drawn_inputs = setup_inputs


def setup_inputs(seed=0):
    import zlib

    import numpy as np

    out = dict(_drawn_inputs(seed))
    spreads = {}
    factors = {}
    for name, (base, spread) in spreads.items():
        noise = np.random.default_rng([zlib.crc32(name.encode()), seed]).standard_normal(out[name].shape)
        drawn = base * np.exp(spread * noise) if base else spread * noise
        out[name] = jnp.asarray(drawn.astype(out[name].dtype))
    for name, factor in factors.items():
        out[name] = (out[name] * factor).astype(out[name].dtype)
    return out
```

```python
from contextlib import ExitStack

import concourse.bass as bass
from concourse import mybir

F32 = mybir.dt.float32
F16 = mybir.dt.float16
I32 = mybir.dt.int32
ALU = mybir.AluOpType
ACT = mybir.ActivationFunctionType
AX_X = mybir.AxisListType.X
RMAX = bass.bass_isa.ReduceOp.max

P = 128
BATCH, CHANNELS, L = 16, 256, 512
HD = 8
HEADS = CHANNELS // HD
LB = L // P
QUAD = 4
GROUPS = HEADS // QUAD
ROWS = QUAD * P
INNER = 1408
IC = INNER // P
GU = 2 * IC
HALF = HD * 8
EXT = HALF + 32
PAIRS = 4 * HALF + 32
ZW = 96
WORDS = 16
LN_EPS = 1e-5
RMS_EPS = 1e-6

UNITS = 2 * IC + 3 * QUAD
DOWN_PARTS = (range(0, 4), range(4, 8), range(8, IC))

SLOTS = [[] for _ in range(UNITS + 2)]
for _q in range(QUAD):
    _b = 7 * _q
    SLOTS[_b] += [("load_ct", _q), ("conv", _q, 0)]
    SLOTS[_b + 1] += [("turn_c", _q + 1)]
    if _q:
        SLOTS[_b + 2] += [("turn_out", _q - 1)]
        SLOTS[_b + 5] += [("turn_x", _q - 1)]
    SLOTS[_b + 2] += [("conv", _q, 1), ("pairs", _q + 1, 0)]
    SLOTS[_b + 3] += [("load_x", _q), ("turn_q", _q + 1), ("pairs", _q + 1, 1)]
    SLOTS[_b + 4] += [("conv", _q, 2)]
    SLOTS[_b + 6] += [("conv", _q, 3), ("stats", _q + 2)]
SLOTS[30] += [("turn_out", QUAD - 1)]
SLOTS[33] += [("turn_x", QUAD - 1)]

BATCHES = [(0, 0, 6), (0, 6, 6), (0, 12, 6), (0, 18, 4), (1, 0, 2), (1, 2, 2)]
PIECES = []
for _n, (_down, _t0, _nt) in enumerate(BATCHES):
    for _t in range(_t0, _t0 + _nt):
        for _c in range(0, IC if _down else LB, 4):
            PIECES.append((_n, _down, _t, _c, min(4, (IC if _down else LB) - _c)))


class Group:

    def __init__(self, number, halved, parity):
        self.n, self.halved, self.parity = number, halved, parity

    def next(self):
        return Group(self.n + 1, self.halved + self.parity, 1 - self.parity)

    def prev(self):
        return Group(self.n - 1, self.halved - 1 + self.parity, 1 - self.parity)

    def head(self, q):
        return self.n * QUAD + q

    def uses(self, q, ring):
        return self.n * (QUAD // ring) + q // ring


def static_group(n):
    return Group(n, n // 2, n % 2)


def wait(eng, sem, count):
    if not isinstance(count, int) or count > 0:
        eng.wait_ge(sem, count)


def flamingo_block(nc, x, ctx, g_xattn, g_ffn, taps, skip, gu_packed, gu_scales, dn_packed, dn_scales,
                   identity, out):
    with ExitStack() as es:
        def sb(name, shape, dt):
            return es.enter_context(nc.sbuf_tensor(name, shape, dt))

        def ps(name, shape, dt=F32):
            return es.enter_context(nc.psum_tensor(name, shape, dt))

        def sem(name):
            return es.enter_context(nc.semaphore(name))

        toeplitz = nc.dram_tensor("toeplitz_taps", [HEADS, 2, P + L], F16, kind="Internal").ap()
        tap_scale = nc.dram_tensor("tap_scale", [HEADS, 1], F32, kind="Internal").ap()

        w_gu = sb("w_gu", [P, 2, LB, 2 * INNER], F16)
        w_dn = sb("w_dn", [P, 2, IC, L], F16)
        ident = sb("ident", [P, P], F32)
        ident16 = sb("ident16", [P, 2, P], F16)
        x_in = sb("x_in", [P, 4, L], F32)
        c_in = sb("c_in", [P, 2, L], F32)
        t_in = sb("t_in", [P, 2, 2, L], F16)
        c_scaled = sb("c_scaled", [P, L], F32)
        q_rows = sb("q_rows", [P, L], F32)
        c_cols = sb("c_cols", [P, LB * 2, EXT], F32)
        q_cols = sb("q_cols", [P, 2, LB * 2, EXT], F32)
        pair32 = sb("pair32", [P, LB * 2, PAIRS], F32)
        pair_hi = sb("pair_hi", [P, 2, LB * 2, PAIRS], F16)
        pair_lo = sb("pair_lo", [P, 2, LB * 2, PAIRS], F16)
        z = sb("z", [P, 2, 8, ZW], F32)
        z1 = sb("z1", [P, 2, 4, HALF], F32)
        z2 = sb("z2", [P, 2, 2, HALF], F32)
        z_wrap = sb("z_wrap", [P, 2, 24], F32)
        o_cols = sb("o_cols", [P, 2, LB, P], F32)
        bn = sb("bn", [P, 2, 6], F32)
        head_small = sb("head_small", [P, 4, 17], F32)
        tap_factor = sb("tap_factor", [P, 2, QUAD], F32)
        x1 = sb("x1", [P, 2, QUAD, L], F32)
        xn_rows = sb("xn_rows", [P, L], F32)
        xn_cols = sb("xn_cols", [P, 2, 2, LB, ROWS], F16)
        silu_g = sb("silu_g", [P, 2, ROWS], F32)
        h32 = sb("h32", [P, 2, ROWS], F32)
        h = sb("h", [P, 2, IC, ROWS], F16)
        square = sb("square", [P, 2, L], F32)
        tile_small = sb("tile_small", [P, 2, 4], F32)
        const = sb("const", [P, 24], F32)
        k_small = sb("k_small", [HEADS, 8], F32)
        scale_gu = sb("scale_gu", [P, GU * LB], F16)
        scale_dn = sb("scale_dn", [P, LB * IC], F16)
        kp = silu_g[0:HEADS].rearrange("p a s -> p (a s)")[:, 0:P + L]
        kp_split = h32[0:HEADS].rearrange("p a s -> p (a s)")[:, 0:P + L].bitcast(F16).rearrange(
            "p (a s) -> p a s", a=2)
        x1_words = x1[:, :, :, :].rearrange("p a q l -> p (a q l)").bitcast(I32)
        n_gu, n_dn = GU * LB * WORDS, LB * IC * WORDS
        packed_gu, packed_dn = x1_words[:, 0:n_gu], x1_words[:, n_gu:n_gu + n_dn]
        diag = x1_words[:, n_gu + n_dn:n_gu + n_dn + 4 * 4 * P // 2].bitcast(F16).rearrange(
            "p (w j o) -> p w j o", w=4, j=4)
        VW = 6 * LB * WORDS
        h_words = h[:, :, :, :].rearrange("p a c s -> p (a c s)").bitcast(I32)
        unpacked = [h_words[:, n * 4 * VW:(n + 1) * 4 * VW] for n in range(3)]
        x_words = xn_cols[:, 1].rearrange("p a c s -> p (a c s)").bitcast(I32)
        signs = [x_words[:, n * VW:(n + 1) * VW] for n in range(2)]
        sizes = [x_words[:, (n + 2) * VW:(n + 3) * VW] for n in range(2)]

        PEAK, CPOW, CREC, MEAN, VAR, VE, RS, QS, QB, RF, MEAN2, VAR2, VE2, RS2, QB2, NEG, NEG2 = range(17)
        (MINUS_HALF, TANH_X, TANH_F, MAX_W, MAX_D, PEAK_W, PEAK_D, POW_W, POW_D, REC_W, REC_D, NORM_W, NORM_D,
         GATE_S, H_S, INV, INV2, EPS3) = range(18)

        def col(n):
            return const[:, n:n + 1]

        pair_bank = [[ps("gate0", [P, ROWS]), ps("up0", [P, ROWS])], [ps("gate1", [P, ROWS]), ps("up1", [P, ROWS])]]
        y_bank = pair_bank[1]
        w_bank = pair_bank[0] + pair_bank[1]
        conv_bank = ps("conv", [P, 2, 512])
        turn_a = ps("turn_a", [P, 512])
        turn_b = ps("turn_b", [P, 512])

        small_in, k_loaded, w_loaded, scales_in = sem("small_in"), sem("k_loaded"), sem("w_loaded"), sem("scales_in")
        x_loaded = [sem(f"x_loaded{n}") for n in range(4)]
        c_loaded = [sem(f"c_loaded{n}") for n in range(2)]
        t_loaded = [sem(f"t_loaded{n}") for n in range(2)]
        factor_loaded = [sem(f"factor_loaded{n}") for n in range(2)]
        taps_stored = sem("taps_stored")
        stored = [sem(f"stored{n}") for n in range(2)]
        zeroed, k_step, w_small, w_peak, tanh_done, ident_cast = (
            sem("zeroed"), sem("k_step"), sem("w_small"), sem("w_peak"), sem("tanh_done"), sem("ident_cast"))
        bits_done, unpack_done, diag_done, w_turned, w_hi, w_lo = (
            sem("bits_done"), sem("unpack_done"), sem("diag_done"), sem("w_turned"), sem("w_hi"), sem("w_lo"))
        c_peak, x_moments, c_clamped, x_aggr, c_pow, var_ready, c_recip = (
            sem("c_peak"), sem("x_moments"), sem("c_clamped"), sem("x_aggr"), sem("c_pow"), sem("var_ready"),
            sem("c_recip"))
        rs_ready, q_scale, q_affine, row_factor = sem("rs_ready"), sem("q_scale"), sem("q_affine"), sem("row_factor")
        c_rows_ready, q_rows_ready, c_turned, q_turned = (
            sem("c_rows_ready"), sem("q_rows_ready"), sem("c_turned"), sem("q_turned"))
        c_cols_ready, q_cols_ready, pairs_ready, pairs_hi, pairs_lo = (
            sem("c_cols_ready"), sem("q_cols_ready"), sem("pairs_ready"), sem("pairs_hi"), sem("pairs_lo"))
        conv_done, z_filled, z1_done, z2_done, wrap_done, o_summed, o_ready = (
            sem("conv_done"), sem("z_filled"), sem("z1_done"), sem("z2_done"), sem("wrap_done"), sem("o_summed"),
            sem("o_ready"))
        out_turned, x1_ready, x1_moments, x1_aggr, var2_ready, rs2_ready, xn_affine = (
            sem("out_turned"), sem("x1_ready"), sem("x1_moments"), sem("x1_aggr"), sem("var2_ready"),
            sem("rs2_ready"), sem("xn_affine"))
        xn_rows_ready, xn_turned, xn_hi, xn_lo = (
            sem("xn_rows_ready"), sem("xn_turned"), sem("xn_hi"), sem("xn_lo"))
        gate_done, up_done, silu_done, h_ready, h_hi, h_lo = (
            sem("gate_done"), sem("up_done"), sem("silu_done"), sem("h_ready"), sem("h_hi"), sem("h_lo"))
        y_done, squared, mean_square, y_rs, y_scale, out_ready = (
            sem("y_done"), sem("squared"), sem("mean_square"), sem("y_rs"), sem("y_scale"), sem("out_ready"))

        def small(q, c, n=1):
            return head_small[:, q % 4, c:c + n]

        def program(group_program, lead):
            lead()
            group_program(static_group(0), True, False, False)
            return group_program

        PAIRED = (GROUPS - 2) // 2

        def run_groups(eng, group_program):
            group_program(static_group(0), True, False, False)
            with eng.Fori(0, PAIRED) as turn:
                group_program(Group(turn * 2 + 1, turn, 1), True, True, False)
                group_program(Group(turn * 2 + 2, turn + 1, 0), True, True, False)
            group_program(static_group(GROUPS - 1), True, True, True)
            group_program(static_group(GROUPS), False, True, True)

        block = es.enter_context(nc.Block())

        @block.sync
        def _(sp):
            def rows_of(tensor, grp, q, half):
                if isinstance(grp.n, int):
                    channels = slice(grp.head(q) * HD, grp.head(q) * HD + HD)
                else:
                    channels = bass.ds(grp.n * (QUAD * HD) + q * HD, HD)
                return tensor[8 * half:8 * half + 8, channels, :].rearrange("b i l -> i b l")

            def load_c(grp, q):
                wait(sp, c_rows_ready, grp.head(q) - 1)
                for half in range(2):
                    sp.dma_start(c_in[64 * half:64 * half + 64, q % 2, :],
                                 rows_of(ctx, grp, q, half)).then_inc(c_loaded[q % 2], 16)

            def load_x(grp, q):
                wait(sp, x1_ready, grp.head(q) - 3)
                for half in range(2):
                    sp.dma_start(x_in[64 * half:64 * half + 64, q % 4, :],
                                 rows_of(x, grp, q, half)).then_inc(x_loaded[q % 4], 16)

            def load_taps(grp, q):
                wait(sp, conv_done, grp.head(q) * LB - LB)
                if isinstance(grp.n, int):
                    first = toeplitz[grp.head(q):grp.head(q) + 1, 0, 1:1 + L]
                else:
                    first = toeplitz[bass.ds(grp.n * QUAD + q, 1), 0, 1:1 + L]
                windows = bass.AP(tensor=first.tensor, offset=first.offset, ap=[[1, P], [P + L, 2], [1, L]])
                sp.dma_start(t_in[:, q % 2, :, :], windows).then_inc(t_loaded[q % 2], 16)

            def load_factor(grp):
                if isinstance(grp.n, int):
                    first = tap_scale[grp.head(0):grp.head(0) + QUAD, 0:1]
                else:
                    first = tap_scale[bass.ds(grp.n * QUAD, QUAD), 0:1]
                everywhere = bass.AP(tensor=first.tensor, offset=first.offset, ap=[[0, P], [1, QUAD]])
                sp.dma_start(tap_factor[:, grp.parity, :], everywhere).then_inc(factor_loaded[grp.parity], 16)

            def store(grp, q):
                sp.wait_ge(out_ready, grp.head(q) + 2)
                for half in range(2):
                    sp.dma_start(rows_of(out, grp, q, half),
                                 x1[64 * half:64 * half + 64, grp.parity, q, :]).then_inc(stored[grp.parity], 16)

            def one_group(grp, attention, feed, last):
                for t in range(UNITS + 2):
                    for stage, q, *_n in SLOTS[t] if attention else []:
                        if stage == "load_ct":
                            if not (last and q + 1 >= QUAD):
                                load_taps(grp, q + 1)
                            if not (last and q + 3 >= QUAD):
                                load_c(grp, q + 3)
                        elif stage == "load_x" and not (last and q + 3 >= QUAD):
                            load_x(grp, q + 3)
                            if q == 0 and not last:
                                load_factor(grp.next())
                    if feed and t >= 27 and (t - 27) % 3 == 0:
                        store(grp.prev(), (t - 27) // 3)
                if feed:
                    store(grp.prev(), QUAD - 1)

            for n in range(2):
                sp.sem_inc(stored[n], 16)
            sp.wait_ge(zeroed, 1)
            sp.dma_start(kp[:, P:], taps).then_inc(k_loaded, 16)
            sp.dma_start(k_small[:, 0:1], skip).then_inc(k_loaded, 16)
            first = static_group(0)
            load_c(first, 0)
            load_x(first, 0)
            sp.dma_start(ident[:, :], identity).then_inc(small_in, 16)
            sp.dma_start(const[:, TANH_X:TANH_X + 1], g_xattn.partition_broadcast(P)).then_inc(small_in, 16)
            sp.dma_start(const[:, TANH_F:TANH_F + 1], g_ffn.partition_broadcast(P)).then_inc(small_in, 16)
            sp.dma_start(scale_gu[:, :], gu_scales).then_inc(scales_in, 16)
            sp.dma_start(scale_dn[:, :], dn_scales).then_inc(scales_in, 16)
            sp.dma_start(packed_gu[:, :], gu_packed).then_inc(w_loaded, 16)
            sp.dma_start(packed_dn[:, :], dn_packed).then_inc(w_loaded, 16)
            load_c(first, 1)
            load_x(first, 1)
            load_x(first, 2)
            sp.wait_ge(k_step, 7)
            sp.dma_start(toeplitz, kp_split[:, :, :]).then_inc(taps_stored, 16)
            sp.dma_start(tap_scale, k_small[:, 3:4]).then_inc(taps_stored, 16)
            sp.wait_ge(taps_stored, 32)
            load_factor(first)
            load_taps(first, 0)
            load_c(first, 2)
            run_groups(sp, one_group)
            for n in range(2):
                sp.wait_ge(stored[n], 2 * 16 * QUAD * (GROUPS // 2) + 16)

        @block.tensor
        def _(pe):
            def turn(bank, src, done):
                for b in range(LB):
                    mm = pe.transpose(bank[:, P * b:P * b + P], src[:, b], ident[:, :])
                mm.then_inc(done, 1)

            def turned_out_before(grp, q):
                return grp.head(q) - (1 if q == 1 else 2)

            def turned_in_before(grp, q, last):
                ahead = 3 if q < QUAD - 1 else 2
                return grp.head(min(q + ahead, QUAD) if last else q + ahead)

            def turn_c(grp, q):
                wait(pe, c_cols_ready, grp.head(q) * 2)
                wait(pe, x1_ready, turned_out_before(grp, q))
                pe.wait_ge(c_rows_ready, grp.head(q) + 1)
                turn(turn_a, c_scaled[:, :].rearrange("p (b t) -> p b t", b=LB), c_turned)

            def turn_q(grp, q):
                wait(pe, q_cols_ready, grp.head(q) * 2)
                wait(pe, xn_lo, turned_out_before(grp, q))
                pe.wait_ge(q_rows_ready, grp.head(q) + 1)
                turn(turn_b, q_rows[:, :].rearrange("p (b t) -> p b t", b=LB), q_turned)

            def turn_out(grp, q, last):
                pe.wait_ge(c_cols_ready, turned_in_before(grp, q, last) * 2)
                wait(pe, x1_ready, grp.head(q))
                pe.wait_ge(o_ready, (grp.head(q) + 1) * LB)
                turn(turn_a, o_cols[:, q % 2], out_turned)

            def turn_x(grp, q, last):
                pe.wait_ge(q_cols_ready, turned_in_before(grp, q, last) * 2)
                wait(pe, xn_lo, grp.head(q))
                pe.wait_ge(xn_rows_ready, grp.head(q) + 1)
                turn(turn_b, xn_rows[:, :].rearrange("p (b t) -> p b t", b=LB), xn_turned)

            def conv(grp, q, n):
                wait(pe, z_filled, (grp.head(q) * LB + n) * 3)
                if n == 0:
                    pe.wait_ge(t_loaded[q % 2], (grp.uses(q, 2) + 1) * 16)
                if n % 2 == 0:
                    pe.wait_ge(pairs_lo, grp.head(q) * 2 + n // 2 + 1)
                for b in range(n + 1):
                    for part, moving in ((0, (pair_hi, pair_lo)), (1, (pair_hi,))):
                        w = t_in[:, q % 2, part, (n - b) * P:(n - b + 1) * P]
                        for m in moving:
                            for half in range(2):
                                mm = pe.matmul(conv_bank[:, half, 0:PAIRS], w, m[:, q % 2, 2 * b + half, :],
                                               start=(b == 0 and part == 0 and m is pair_hi),
                                               stop=(b == n and part == 1))
                mm.then_inc(conv_done, 1)

            def products(bank, steps):
                for k, (sta, mov) in enumerate(steps):
                    pe.matmul(bank, sta(0), mov(0), start=(k == 0), stop=False)
                    pe.matmul(bank, sta(0), mov(1), start=False, stop=False)
                    mm = pe.matmul(bank, sta(1), mov(0), start=False, stop=(k == len(steps) - 1))
                return mm

            def gate_or_up(grp, u, up):
                f = grp.n * IC
                if u == 0 and not up:
                    pe.wait_ge(xn_lo, grp.head(QUAD))
                if u == 1:
                    pe.wait_ge(out_ready, grp.head(0) + 1)
                elif u > 1 and up:
                    pe.wait_ge(h_ready, f + u - 1)
                elif u > 1:
                    pe.wait_ge(silu_done, f + u - 1)
                o = (IC * up + u) * P
                steps = [(lambda part, b=b: w_gu[:, part, b, o:o + P],
                          lambda part, b=b: xn_cols[:, grp.parity, part, b, :]) for b in range(LB)]
                products(pair_bank[u % 2][up][:, :], steps).then_inc(up_done if up else gate_done, 1)

            def down(grp, s, part):
                f = grp.n * IC
                if part == 0:
                    if s == 0:
                        pe.wait_ge(silu_done, f + IC - 1)
                    elif s == 1:
                        pe.wait_ge(h_ready, f + IC - 1)
                    else:
                        pe.wait_ge(out_ready, grp.head(s))
                for c in DOWN_PARTS[part]:
                    if s == 0:
                        pe.wait_ge(h_lo, f + c + 1)
                    bank = y_bank[s % 2][:, :]
                    rows = slice(s * P, s * P + P)
                    pe.matmul(bank, h[:, 0, c, rows], w_dn[:, 0, c, :], start=(c == 0), stop=False)
                    pe.matmul(bank, h[:, 0, c, rows], w_dn[:, 1, c, :], start=False, stop=False)
                    mm = pe.matmul(bank, h[:, 1, c, rows], w_dn[:, 0, c, :], start=False, stop=(c == IC - 1))
                if part == 2:
                    mm.then_inc(y_done, 1)

            def one_group(grp, attention, feed, last):
                for t in range(UNITS):
                    for stage, q, *n in SLOTS[t] if attention else []:
                        if stage == "conv":
                            conv(grp, q, n[0])
                        elif stage == "turn_c" and not (last and q >= QUAD):
                            turn_c(grp, q)
                        elif stage == "turn_q" and not (last and q >= QUAD):
                            turn_q(grp, q)
                        elif stage == "turn_out":
                            turn_out(grp, q, last)
                        elif stage == "turn_x":
                            turn_x(grp, q, last)
                    if feed and t < 2 * IC:
                        gate_or_up(grp.prev(), t // 2, t % 2)
                    elif feed:
                        down(grp.prev(), (t - 2 * IC) // 3, (t - 2 * IC) % 3)

            pe.wait_ge(small_in, 48)
            for w, (batch, is_down, tile, c0, nc_) in enumerate(PIECES):
                if w >= 4:
                    pe.wait_ge(w_lo, w - 3)
                pe.wait_ge(unpack_done, batch + 1)
                pe.wait_ge(diag_done, w + 1)
                values = unpacked[batch % 3].bitcast(F16)
                t0 = BATCHES[batch][1]
                for j in range(nc_):
                    c = (tile - t0) * (IC if is_down else LB) + c0 + j
                    mm = pe.matmul(w_bank[w % 4][:, P * j:P * j + P], values[:, P * c:P * c + P], diag[:, w % 4, j, :],
                                   start=True, stop=True)
                mm.then_inc(w_turned, 1)
            turn_c(static_group(0), 0)
            turn_q(static_group(0), 0)
            run_groups(pe, one_group)

        @block.scalar
        def _(act):
            def scale_c(grp, q):
                wait(act, c_turned, grp.head(q))
                act.wait_ge(c_recip, grp.head(q) + 1)
                act.activation(c_scaled[:, :].rearrange("p (b t) -> p b t", b=LB)[:, :, ::-1],
                               c_in[:, q % 2, :].rearrange("p (b t) -> p b t", b=LB),
                               ACT.Copy, scale=small(q, CREC)).then_inc(c_rows_ready, 1)

            def make_q(grp, q):
                wait(act, q_turned, grp.head(q))
                act.wait_ge(q_affine, grp.head(q) + 1)
                act.activation(q_rows[:, :], x_in[:, q % 4, :], ACT.Identity, scale=small(q, QS),
                               bias=small(q, QB)).then_inc(q_rows_ready, 1)

            def extend(dst, bank, done, scale):
                src = bank[:, :].rearrange("p (g c) -> p g c", c=HALF)
                act.activation(dst[:, :, 0:HALF], src, ACT.Copy, scale=scale).then_inc(done, 1)
                act.activation(dst[:, :, HALF:EXT], src[:, :, 0:EXT - HALF], ACT.Copy, scale=scale).then_inc(done, 1)

            def take_c(grp, q):
                wait(act, pairs_ready, grp.head(q) * 4)
                act.wait_ge(c_turned, grp.head(q) + 1)
                extend(c_cols, turn_a, c_cols_ready, 32.0)

            def take_q(grp, q):
                wait(act, z_filled, (grp.head(q) - 1) * LB * 3)
                act.wait_ge(q_turned, grp.head(q) + 1)
                extend(q_cols[:, q % 2], turn_b, q_cols_ready, 1.0)

            def pairs_high(grp, q, n):
                if n == 0:
                    wait(act, conv_done, (grp.head(q) - 1) * LB)
                act.wait_ge(pairs_ready, grp.head(q) * 4 + 2 * n + 2)
                act.activation(pair_hi[:, q % 2, 4 * n:4 * n + 4, :], pair32[:, 4 * n:4 * n + 4, :],
                               ACT.Copy).then_inc(pairs_hi, 1)

            def normalise(grp, q):
                wait(act, xn_turned, grp.head(q))
                act.wait_ge(xn_affine, grp.head(q) + 1)
                act.activation(xn_rows[:, :].rearrange("p (b k m) -> p b m k", b=LB, k=4),
                               x1[:, grp.parity, q, :].rearrange("p (b m k) -> p b m k", b=LB, k=4),
                               ACT.Identity, scale=small(q, RS2),
                               bias=small(q, QB2)).then_inc(xn_rows_ready, 1)

            def x_high(grp, q):
                act.wait_ge(xn_turned, grp.head(q) + 1)
                act.activation(xn_cols[:, grp.parity, 0, :, q * P:q * P + P],
                               turn_b[:, :].rearrange("p (b r) -> p b r", b=LB), ACT.Copy).then_inc(xn_hi, 1)

            def silu(grp, u):
                f = grp.n * IC
                if u >= 2:
                    act.wait_ge(h_ready, f + u - 1)
                act.wait_ge(gate_done, f + u + 1)
                act.activation(silu_g[:, u % 2, :], pair_bank[u % 2][0][:, :], ACT.Silu,
                               scale=col(GATE_S)).then_inc(silu_done, 1)

            def h_high(grp, u):
                f = grp.n * IC
                act.wait_ge(h_ready, f + u + 1)
                act.activation(h[:, 0, u, :], h32[:, u % 2, :], ACT.Copy).then_inc(h_hi, 1)

            def square_y(grp, s):
                if s >= 2:
                    act.wait_ge(mean_square, grp.head(s) - 1)
                act.wait_ge(y_done, grp.head(s) + 1)
                act.activation(square[:, s % 2, :], y_bank[s % 2][:, :], ACT.Square,
                               scale=L ** -0.5, accum_out=tile_small[:, s % 2, 0:1]).then_inc(squared, 2)

            def one_group(grp, attention, feed, last):
                for t in range(UNITS + 2):
                    if feed:
                        if t % 2 == 1 and t < 2 * IC:
                            silu(grp.prev(), t // 2)
                        if t % 2 == 0 and 2 <= t <= 2 * IC:
                            h_high(grp.prev(), t // 2 - 1)
                        if t >= 25 and (t - 25) % 3 == 0:
                            square_y(grp.prev(), (t - 25) // 3)
                    for stage, q, *n in SLOTS[t] if attention else []:
                        if last and q >= QUAD:
                            continue
                        if stage == "turn_c":
                            take_c(grp, q)
                        elif stage == "turn_q":
                            take_q(grp, q)
                        elif stage == "pairs":
                            pairs_high(grp, q, n[0])
                        elif stage == "turn_out":
                            normalise(grp, q)
                        elif stage == "turn_x":
                            x_high(grp, q)
                        elif stage == "stats":
                            scale_c(grp, q)
                            make_q(grp, q)

            act.wait_ge(small_in, 48)
            act.activation(col(TANH_X), col(TANH_X), ACT.Tanh).then_inc(tanh_done, 1)
            act.activation(col(TANH_F), col(TANH_F), ACT.Tanh).then_inc(tanh_done, 1)
            first = static_group(0)
            scale_c(first, 0)
            make_q(first, 0)
            act.wait_ge(w_small, 10)
            for w, (batch, is_down, tile, c0, nc_) in enumerate(PIECES):
                act.wait_ge(w_turned, w + 1)
                dst = w_dn[:, 0, c0:c0 + nc_, tile * P:tile * P + P] if is_down else w_gu[:, 0, :, tile * P:tile * P + P]
                act.activation(dst, w_bank[w % 4][:, 0:nc_ * P].rearrange("p (c o) -> p c o", o=P), ACT.Copy,
                               scale=col(NORM_D if is_down else NORM_W)).then_inc(w_hi, 1)
            take_c(first, 0)
            take_q(first, 0)
            pairs_high(first, 0, 0)
            pairs_high(first, 0, 1)
            scale_c(first, 1)
            make_q(first, 1)
            run_groups(act, one_group)

        @block.gpsimd
        def _(pool):
            def row_scalars(grp, q):
                n = grp.head(q)
                pool.wait_ge(var_ready, 2 * n + 2)
                pool.tensor_tensor(small(q, RS), small(q, VE), col(MINUS_HALF), ALU.pow).then_inc(rs_ready, 1)
                if q % 4 == 0:
                    home = grp if q == 0 else grp.next()
                    pool.wait_ge(factor_loaded[home.parity], (home.halved + 1) * 16)
                pool.wait_ge(c_recip, n + 1)
                parity = grp.parity if q < QUAD else 1 - grp.parity
                pool.tensor_tensor(small(q, RF), small(q, CPOW), tap_factor[:, parity, q % 4:q % 4 + 1],
                                   ALU.mult).then_inc(row_factor, 1)
                pool.wait_ge(rs_ready, n + 1)
                pool.tensor_tensor(small(q, QS), small(q, RS), small(q, CPOW), ALU.mult).then_inc(q_scale, 1)
                pool.wait_ge(q_scale, n + 1)
                pool.tensor_tensor(small(q, QB), small(q, NEG), small(q, QS), ALU.mult).then_inc(q_affine, 1)

            def norm_scalars(grp, q):
                n = grp.head(q)
                pool.wait_ge(var2_ready, 2 * n + 2)
                pool.tensor_tensor(small(q, RS2), small(q, VE2), col(MINUS_HALF), ALU.pow).then_inc(rs2_ready, 1)
                pool.wait_ge(rs2_ready, n + 1)
                pool.tensor_tensor(small(q, QB2), small(q, NEG2), small(q, RS2), ALU.mult).then_inc(xn_affine, 1)

            def y_scalars(grp, s):
                n = grp.head(s)
                pool.wait_ge(squared, 2 * n + 2)
                pool.tensor_tensor(tile_small[:, s % 2, 1:2], tile_small[:, s % 2, 0:1], col(EPS3),
                                   ALU.add).then_inc(mean_square, 1)
                pool.wait_ge(mean_square, n + 1)
                pool.tensor_tensor(tile_small[:, s % 2, 2:3], tile_small[:, s % 2, 1:2], col(MINUS_HALF),
                                   ALU.pow).then_inc(y_rs, 1)
                if s >= 2:
                    pool.wait_ge(out_ready, n)
                pool.wait_ge(y_rs, n + 1)
                pool.tensor_tensor(tile_small[:, s % 2, 3:4], tile_small[:, s % 2, 2:3], col(TANH_F),
                                   ALU.mult).then_inc(y_scale, 1)

            def one_group(grp, attention, feed, last):
                for t in range(UNITS + 2):
                    if feed and t >= 25 and (t - 25) % 3 == 0:
                        y_scalars(grp.prev(), (t - 25) // 3)
                    for stage, q, *_n in SLOTS[t] if attention else []:
                        if last and q >= QUAD:
                            continue
                        if stage == "stats":
                            row_scalars(grp, q)
                        elif stage == "turn_out":
                            norm_scalars(grp, q)

            pool.wait_ge(w_small, 2)
            pool.partition_all_reduce(col(PEAK_W), col(MAX_W), P, RMAX).then_inc(w_peak, 1)
            pool.partition_all_reduce(col(PEAK_D), col(MAX_D), P, RMAX).then_inc(w_peak, 1)
            first = static_group(0)
            row_scalars(first, 0)
            pool.wait_ge(ident_cast, 2)
            for w, (batch, is_down, tile, c0, nc_) in enumerate(PIECES):
                if w >= 4:
                    pool.wait_ge(w_turned, w - 3)
                for j in range(nc_):
                    scales, c = (scale_dn, tile * IC + c0 + j) if is_down else (scale_gu, tile * LB + j)
                    ins = pool.tensor_scalar(diag[:, w % 4, j, :], ident16[:, is_down, :], scales[:, c:c + 1], 1.0, ALU.mult,
                                             ALU.mult)
                ins.then_inc(diag_done, 1)
            row_scalars(first, 1)
            run_groups(pool, one_group)

        @block.vector
        def _(dve):
            def stats(grp, q):
                n = grp.head(q)
                dve.wait_ge(c_loaded[q % 2], (grp.uses(q, 2) + 1) * 32)
                dve.tensor_reduce(small(q, PEAK), c_in[:, q % 2, :], AX_X, ALU.max,
                                  apply_absolute_value=True).then_inc(c_peak, 1)
                dve.wait_ge(x_loaded[q % 4], (grp.uses(q, 4) + 1) * 32)
                dve.bn_stats(bn[:, 0, :], x_in[:, q % 4, :]).then_inc(x_moments, 1)
                dve.wait_ge(x_moments, n + 1)
                dve.wait_ge(c_peak, n + 1)
                dve.tensor_scalar(small(q, PEAK), small(q, PEAK), 2.0 ** -60, None, ALU.max).then_inc(c_clamped, 1)
                dve.bn_aggr(small(q, MEAN, 2), bn[:, 0, :]).then_inc(x_aggr, 1)
                dve.wait_ge(c_clamped, n + 1)
                dve.tensor_scalar(small(q, CPOW).bitcast(I32), small(q, PEAK).bitcast(I32), 0x7F800000, None,
                                  ALU.bitwise_and).then_inc(c_pow, 1)
                dve.wait_ge(x_aggr, n + 1)
                dve.tensor_scalar(small(q, NEG), small(q, MEAN), -1.0, None, ALU.mult).then_inc(var_ready, 1)
                dve.tensor_scalar(small(q, VE), small(q, VAR), LN_EPS, 1024.0, ALU.add, ALU.mult).then_inc(var_ready, 1)
                dve.wait_ge(c_pow, n + 1)
                dve.reciprocal(small(q, CREC), small(q, CPOW)).then_inc(c_recip, 1)

            def pairs(grp, q, n):
                if n == 0:
                    wait(dve, pairs_hi, grp.head(q) * 2)
                    wait(dve, pairs_lo, grp.head(q) * 2)
                    dve.wait_ge(c_cols_ready, grp.head(q) * 2 + 2)
                g = slice(4 * n, 4 * n + 4)
                first = c_cols[:, g, 0:HALF]
                dve.tensor_tensor(pair32[:, g, 0:4 * HALF].rearrange("p g (d c) -> p g d c", d=4),
                                  spread(first, 0, 4), spread(first, 8, 4), ALU.mult).then_inc(pairs_ready, 1)
                dve.tensor_tensor(pair32[:, g, 4 * HALF:PAIRS], c_cols[:, g, 0:32], c_cols[:, g, 32:64],
                                  ALU.mult).then_inc(pairs_ready, 1)

            def pairs_low(grp, q, n):
                dve.wait_ge(pairs_hi, grp.head(q) * 2 + n + 1)
                g = slice(4 * n, 4 * n + 4)
                dve.tensor_tensor(pair_lo[:, q % 2, g, :], pair32[:, g, :], pair_hi[:, q % 2, g, :],
                                  ALU.subtract).then_inc(pairs_lo, 1)

            def spread(ap, step, count):
                a = [list(pair) for pair in ap.ap]
                return bass.AP(tensor=ap.tensor, offset=ap.offset, ap=[a[0], a[1], [step, count], a[2]])

            def weigh(grp, q, n):
                m = grp.head(q) * LB + n
                if n == 0:
                    dve.wait_ge(q_cols_ready, grp.head(q) * 2 + 2)
                    wait(dve, out_turned, grp.head(q) - 1)
                wait(dve, z1_done, m)
                wait(dve, wrap_done, m)
                dve.wait_ge(conv_done, m + 1)
                y = conv_bank[:, :, 0:HALF]
                ql = q_cols[:, q % 2, 2 * n:2 * n + 2, 0:HALF]
                dve.tensor_tensor(spread(z[:, :, 0, 0:HALF], ZW + 8, 4), spread(y, HALF, 4), spread(ql, 0, 4),
                                  ALU.mult).then_inc(z_filled, 1)
                dve.tensor_tensor(z[:, :, 4:7, 0:HALF], spread(conv_bank[:, :, HALF:2 * HALF], HALF, 3),
                                  spread(q_cols[:, q % 2, 2 * n:2 * n + 2, 8:8 + HALF], 8, 3),
                                  ALU.mult).then_inc(z_filled, 1)
                dve.tensor_tensor(z[:, :, 7, 0:HALF].rearrange("p g (k c) -> p g k c", k=2),
                                  spread(conv_bank[:, :, 4 * HALF:PAIRS], 0, 2),
                                  spread(q_cols[:, q % 2, 2 * n:2 * n + 2, 32:64], 32, 2),
                                  ALU.mult).then_inc(z_filled, 1)
                dve.wait_ge(z_filled, 3 * m + 3)
                wait(dve, z2_done, m)
                dve.tensor_tensor(z1[:, :, :, :], z[:, :, 0:4, 0:HALF], z[:, :, 4:8, 0:HALF],
                                  ALU.add).then_inc(z1_done, 1)
                wait(dve, o_ready, m)
                dve.tensor_reduce(z_wrap[:, :, :], z[:, :, 1:4, HALF:HALF + 24].rearrange("p g d c -> p g c d"), AX_X,
                                  ALU.add).then_inc(wrap_done, 1)
                dve.wait_ge(z1_done, m + 1)
                dve.tensor_tensor(z2[:, :, :, :], z1[:, :, 0:2, :], z1[:, :, 2:4, :], ALU.add).then_inc(z2_done, 1)
                dve.wait_ge(z2_done, m + 1)
                o = o_cols[:, q % 2, n, :].rearrange("p (g c) -> p g c", g=2)
                dve.tensor_tensor(o, z2[:, :, 0, :], z2[:, :, 1, :], ALU.add).then_inc(o_summed, 1)
                dve.wait_ge(wrap_done, m + 1)
                dve.wait_ge(o_summed, m + 1)
                dve.tensor_tensor(o[:, :, 0:24], o[:, :, 0:24], z_wrap[:, :, :], ALU.add).then_inc(o_ready, 1)

            def add_attention(grp, q):
                n = grp.head(q)
                if q == 0:
                    dve.wait_ge(stored[grp.parity], grp.halved * (2 * 16 * QUAD) + 16)
                dve.wait_ge(row_factor, n + 1)
                dve.wait_ge(out_turned, n + 1)
                dve.scalar_tensor_tensor(x1[:, grp.parity, q, :], turn_a[:, :], small(q, RF), x_in[:, q % 4, :],
                                         ALU.mult, ALU.add).then_inc(x1_ready, 1)
                dve.wait_ge(x1_ready, n + 1)
                dve.bn_stats(bn[:, 1, :], x1[:, grp.parity, q, :]).then_inc(x1_moments, 1)
                dve.wait_ge(x1_moments, n + 1)
                dve.tensor_copy(small(q, VE2), small(q, VE2))
                dve.bn_aggr(small(q, MEAN2, 2), bn[:, 1, :]).then_inc(x1_aggr, 1)
                dve.wait_ge(x1_aggr, n + 1)
                dve.tensor_scalar(small(q, NEG2), small(q, MEAN2), -1.0, None, ALU.mult).then_inc(var2_ready, 1)
                dve.tensor_scalar(small(q, VE2), small(q, VAR2), LN_EPS, 2.0 ** -16, ALU.add,
                                  ALU.mult).then_inc(var2_ready, 1)

            def x_low(grp, q):
                dve.wait_ge(xn_hi, grp.head(q) + 1)
                dve.tensor_tensor(xn_cols[:, grp.parity, 1, :, q * P:q * P + P],
                                  turn_b[:, :].rearrange("p (b r) -> p b r", b=LB),
                                  xn_cols[:, grp.parity, 0, :, q * P:q * P + P], ALU.subtract).then_inc(xn_lo, 1)

            def make_h(grp, u):
                f = grp.n * IC
                if u >= 2:
                    dve.wait_ge(h_hi, f + u - 1)
                dve.wait_ge(up_done, f + u + 1)
                dve.wait_ge(silu_done, f + u + 1)
                dve.scalar_tensor_tensor(h32[:, u % 2, :], pair_bank[u % 2][1][:, :], col(H_S), silu_g[:, u % 2, :],
                                         ALU.mult, ALU.mult).then_inc(h_ready, 1)

            def h_low(grp, u):
                dve.wait_ge(h_hi, grp.n * IC + u + 1)
                dve.tensor_tensor(h[:, 1, u, :], h32[:, u % 2, :], h[:, 0, u, :], ALU.subtract).then_inc(h_lo, 1)

            def finish(grp, s):
                dve.wait_ge(y_scale, grp.head(s) + 1)
                rows = x1[:, grp.parity, s, :]
                dve.scalar_tensor_tensor(rows, y_bank[s % 2][:, :], tile_small[:, s % 2, 3:4], rows, ALU.mult,
                                         ALU.add).then_inc(out_ready, 1)

            def one_group(grp, attention, feed, last):
                for t in range(UNITS + 2):
                    if feed:
                        if t % 2 == 0 and 2 <= t <= 2 * IC:
                            make_h(grp.prev(), t // 2 - 1)
                        if t % 2 == 1 and 3 <= t <= 2 * IC + 1:
                            h_low(grp.prev(), (t - 3) // 2)
                        if t >= 26 and (t - 26) % 3 == 0:
                            finish(grp.prev(), (t - 26) // 3)
                    for stage, q, *n in SLOTS[t] if attention else []:
                        if stage == "conv":
                            weigh(grp, q, n[0])
                            if n[0] == 2 and not (last and q + 1 >= QUAD):
                                pairs_low(grp, q + 1, 0)
                                pairs_low(grp, q + 1, 1)
                        elif last and q >= QUAD:
                            continue
                        elif stage == "pairs":
                            pairs(grp, q, n[0])
                        elif stage == "turn_out":
                            add_attention(grp, q)
                        elif stage == "turn_x":
                            x_low(grp, q)
                        elif stage == "stats":
                            stats(grp, q)

            dve.memset(kp[:, 0:P], 0.0).then_inc(zeroed, 1)
            dve.memset(const[:, MINUS_HALF:MINUS_HALF + 1], -0.5).then_inc(zeroed, 1)
            dve.memset(z[:, :, :, :], 0.0).then_inc(zeroed, 1)
            dve.memset(head_small[:, :, :], 0.0).then_inc(zeroed, 1)
            dve.wait_ge(zeroed, 4)
            dve.wait_ge(k_loaded, 32)
            dve.tensor_tensor(kp[:, P:P + 1], kp[:, P:P + 1], k_small[:, 0:1], ALU.add).then_inc(k_step, 1)
            dve.wait_ge(k_step, 1)
            dve.tensor_reduce(k_small[:, 1:2], kp[:, P:], AX_X, ALU.max, apply_absolute_value=True).then_inc(k_step, 1)
            dve.wait_ge(k_step, 2)
            dve.tensor_scalar(k_small[:, 2:3], k_small[:, 1:2], 2.0 ** -60, None, ALU.max).then_inc(k_step, 1)
            dve.wait_ge(k_step, 3)
            dve.tensor_scalar(k_small[:, 4:5].bitcast(I32), k_small[:, 2:3].bitcast(I32), 0x7F800000, None,
                              ALU.bitwise_and).then_inc(k_step, 1)
            dve.wait_ge(k_step, 4)
            dve.reciprocal(k_small[:, 5:6], k_small[:, 4:5]).then_inc(k_step, 1)
            dve.wait_ge(tanh_done, 2)
            dve.tensor_scalar(k_small[:, 3:4], k_small[:, 4:5], const[0:HEADS, TANH_X:TANH_X + 1], 2.0 ** -10, ALU.mult,
                              ALU.mult).then_inc(k_step, 1)
            dve.wait_ge(k_step, 6)
            dve.tensor_scalar(kp[:, :], kp[:, :], k_small[:, 5:6], 32.0, ALU.mult, ALU.mult).then_inc(bits_done, 1)
            dve.wait_ge(bits_done, 1)
            dve.tensor_copy(kp_split[:, 0, :], kp[:, :]).then_inc(bits_done, 1)
            dve.wait_ge(bits_done, 2)
            dve.tensor_tensor(kp_split[:, 1, :], kp[:, :], kp_split[:, 0, :], ALU.subtract).then_inc(k_step, 1)

            dve.wait_ge(scales_in, 32)
            dve.tensor_reduce(col(MAX_W), scale_gu[:, :], AX_X, ALU.max, apply_absolute_value=True).then_inc(w_small, 1)
            dve.tensor_reduce(col(MAX_D), scale_dn[:, :], AX_X, ALU.max, apply_absolute_value=True).then_inc(w_small, 1)
            first = static_group(0)
            stats(first, 0)
            dve.wait_ge(small_in, 48)
            dve.tensor_copy(ident16[:, 1, :], ident[:, :]).then_inc(ident_cast, 1)
            dve.tensor_copy(ident16[:, 0, :].rearrange("p (k m) -> p k m", k=4),
                            ident[:, :].rearrange("p (m k) -> p k m", k=4)).then_inc(ident_cast, 1)
            dve.wait_ge(w_peak, 2)
            peaks, powers, recips = (const[:, c:c + 2] for c in (PEAK_W, POW_W, REC_W))
            dve.tensor_scalar(peaks, peaks, 2.0 ** -24, None, ALU.max).then_inc(w_small, 1)
            dve.wait_ge(w_small, 3)
            dve.tensor_scalar(powers.bitcast(I32), peaks.bitcast(I32), 0x7F800000, None,
                              ALU.bitwise_and).then_inc(w_small, 1)
            dve.wait_ge(w_small, 4)
            dve.reciprocal(recips, powers).then_inc(w_small, 1)
            dve.tensor_scalar(col(GATE_S), col(POW_W), 2.0 ** -8, None, ALU.mult).then_inc(w_small, 1)
            dve.wait_ge(w_small, 6)
            dve.tensor_scalar(const[:, NORM_W:NORM_W + 2], recips, 2.0 ** 14, None, ALU.mult).then_inc(w_small, 1)
            dve.tensor_scalar(col(H_S), col(REC_W), 2.0 ** -18, None, ALU.mult).then_inc(w_small, 1)
            dve.tensor_scalar(col(INV), col(REC_W), col(REC_W), col(REC_D), ALU.mult, ALU.mult).then_inc(w_small, 1)
            dve.wait_ge(w_small, 9)
            dve.tensor_scalar(col(INV2), col(INV), 2.0 ** -10, None, ALU.mult).then_inc(w_small, 1)
            dve.wait_ge(w_small, 10)
            dve.tensor_scalar(col(EPS3), col(INV2), col(INV2), RMS_EPS, ALU.mult, ALU.mult).then_inc(w_small, 1)
            dve.wait_ge(w_small, 11)

            bits = [2]

            def unpack(batch):
                is_down, t0, nt = BATCHES[batch]
                per_tile = (IC if is_down else LB) * WORDS
                n = nt * per_tile
                words = (packed_dn if is_down else packed_gu)[:, t0 * per_tile:t0 * per_tile + n]
                if batch >= 3:
                    done = max(w for w, piece in enumerate(PIECES) if piece[0] == batch - 3) + 1
                    dve.wait_ge(w_turned, done)
                for k in range(4):
                    sign, size = signs[k % 2][:, 0:n], sizes[k % 2][:, 0:n]
                    shift = (ALU.logical_shift_left, 9 - 4 * k) if k < 3 else (ALU.logical_shift_right, 3)
                    dve.tensor_scalar(sign, words, 12 - 4 * k, -0x7FFF8000, ALU.logical_shift_left,
                                      ALU.bitwise_and).then_inc(bits_done, 1)
                    dve.tensor_scalar(size, words, shift[1], 0x0E000E00, shift[0], ALU.bitwise_and).then_inc(bits_done, 1)
                    bits[0] += 2
                    dve.wait_ge(bits_done, bits[0])
                    values = unpacked[batch % 3][:, 0:4 * n].rearrange("p (c k j) -> p c k j", k=4, j=WORDS)[:, :, k, :]
                    ins = dve.tensor_tensor(values, sign.rearrange("p (c j) -> p c j", j=WORDS),
                                            size.rearrange("p (c j) -> p c j", j=WORDS), ALU.bitwise_or)
                    ins.then_inc(bits_done, 1)
                    bits[0] += 1
                dve.wait_ge(bits_done, bits[0])
                dve.sem_inc(unpack_done, 1)

            dve.wait_ge(w_loaded, 32)
            unpack(0)
            for batch in range(len(BATCHES)):
                if batch + 1 < len(BATCHES):
                    unpack(batch + 1)
                for w, (at, is_down, tile, c0, nc_) in enumerate(PIECES):
                    if at != batch:
                        continue
                    dve.wait_ge(w_hi, w + 1)
                    cols = slice(tile * P, tile * P + P)
                    hi, lo = ((w_dn[:, s, c0:c0 + nc_, cols] if is_down else w_gu[:, s, :, cols]) for s in range(2))
                    dve.scalar_tensor_tensor(lo, w_bank[w % 4][:, 0:nc_ * P].rearrange("p (c o) -> p c o", o=P),
                                             col(NORM_D if is_down else NORM_W), hi, ALU.mult,
                                             ALU.subtract).then_inc(w_lo, 1)
            dve.sem_inc(out_ready, 1)
            pairs(first, 0, 0)
            pairs(first, 0, 1)
            pairs_low(first, 0, 0)
            pairs_low(first, 0, 1)
            stats(first, 1)
            run_groups(dve, one_group)


def kernel(x, ctx_2048, g_xattn, g_ffn, L0_xattn_ssm_kernel, L0_xattn_D, L0_ffn_gate_up_packed, L0_ffn_gate_up_scales,
           L0_ffn_down_packed, L0_ffn_down_scales):
    import numpy as np
    import concourse.bacc as bacc
    from concourse.bass_utils import run_bass_kernel_spmd

    def packed_tiles(words):
        words = np.asarray(words)
        return np.ascontiguousarray(words.reshape(-1, P, words.shape[1]).transpose(1, 0, 2).reshape(P, -1))

    def scale_tiles(scales):
        scales = np.asarray(scales)
        return np.ascontiguousarray(scales.reshape(scales.shape[0], -1, P).transpose(2, 1, 0).reshape(P, -1))

    arrays = {
        "x": np.ascontiguousarray(x),
        "ctx": np.ascontiguousarray(ctx_2048),
        "g_xattn": np.ascontiguousarray(g_xattn),
        "g_ffn": np.ascontiguousarray(g_ffn),
        "taps": np.ascontiguousarray(L0_xattn_ssm_kernel),
        "skip": np.ascontiguousarray(L0_xattn_D).reshape(HEADS, 1),
        "gu_packed": packed_tiles(L0_ffn_gate_up_packed),
        "gu_scales": scale_tiles(L0_ffn_gate_up_scales),
        "dn_packed": packed_tiles(L0_ffn_down_packed),
        "dn_scales": scale_tiles(L0_ffn_down_scales),
        "identity": np.eye(P, dtype=np.float32),
    }
    nc = bacc.Bacc("TRN2", target_bir_lowering=False, num_devices=1)
    aps = [nc.dram_tensor(n, a.shape, mybir.dt.from_np(a.dtype), kind="ExternalInput").ap() for n, a in arrays.items()]
    out = nc.dram_tensor("out", (BATCH, CHANNELS, L), F32, kind="ExternalOutput").ap()
    flamingo_block(nc, *aps, out)
    result = run_bass_kernel_spmd(nc, [arrays], core_ids=[0])
    return result.results[0]["out"]
```

```python
from contextlib import ExitStack

import concourse.bass as bass
from concourse import mybir

F32 = mybir.dt.float32
F16 = mybir.dt.float16
I32 = mybir.dt.int32
ALU = mybir.AluOpType
ACT = mybir.ActivationFunctionType
AX_X = mybir.AxisListType.X
RMAX = bass.bass_isa.ReduceOp.max

P = 128
BATCH, CHANNELS, L = 16, 256, 512
HD = 8
HEADS = CHANNELS // HD
LB = L // P
QUAD = 4
FIRST = 2
GROUPS = (HEADS - FIRST) // QUAD + 2
ROWS = QUAD * P
INNER = 1408
IC = INNER // P
GU = 2 * IC
HALF = HD * 8
EXT = HALF + 32
PAIRS = 4 * HALF + 32
ZW = 96
WORDS = 16
LN_EPS = 1e-5
RMS_EPS = 1e-6

UNITS = 2 * IC + 3 * QUAD
DOWN_PARTS = (range(0, 4), range(4, 8), range(8, IC))

SLOTS = [[] for _ in range(UNITS + 3)]
for _q in range(QUAD):
    _b = 7 * _q
    SLOTS[_b] += [("load_ct", _q), ("conv", _q, 0)]
    SLOTS[_b + 1] += [("load_x", _q), ("turn_c", _q + 1)]
    SLOTS[_b + 2] += [("conv", _q, 1), ("pairs", _q + 1, 0)]
    SLOTS[_b + 3] += [("turn_q", _q + 1), ("pairs", _q + 1, 1)]
    SLOTS[_b + 4] += [("conv", _q, 2)]
    SLOTS[_b + 5] += [("stats", _q + 2)]
    SLOTS[_b + 6] += [("conv", _q, 3)]
    if _q:
        SLOTS[_b + 3] += [("turn_out", _q - 1)]
        SLOTS[_b + 6] += [("turn_x", _q - 1)]
SLOTS[30] += [("turn_out", QUAD - 1)]
SLOTS[33] += [("turn_x", QUAD - 1)]

BATCHES = [(0, 0, 6), (0, 6, 6), (0, 12, 6), (0, 18, 4), (1, 0, 2), (1, 2, 2)]
PIECES = []
for _n, (_down, _t0, _nt) in enumerate(BATCHES):
    for _t in range(_t0, _t0 + _nt):
        for _c in range(0, IC if _down else LB, 4):
            PIECES.append((_n, _down, _t, _c, min(4, (IC if _down else LB) - _c)))


FIRST_PIECES = [next(piece for piece in PIECES if piece[0] == _n) for _n in range(len(BATCHES))]

START = 7 * (QUAD - FIRST) - 6
PIECE_SLOTS = range(START + 2, UNITS - 3)


def pieces_at(t):
    if t not in PIECE_SLOTS:
        return ()
    n = t - PIECE_SLOTS[0]
    return range(n * len(PIECES) // len(PIECE_SLOTS), (n + 1) * len(PIECES) // len(PIECE_SLOTS))


class Group:

    def __init__(self, number, halved, parity):
        self.n, self.halved, self.parity = number, halved, parity

    def next(self):
        return Group(self.n + 1, self.halved + self.parity, 1 - self.parity)

    def prev(self):
        return Group(self.n - 1, self.halved - 1 + self.parity, 1 - self.parity)

    def head(self, q):
        return self.n * QUAD + (q - (QUAD - FIRST))

    def exists(self, q):
        return not isinstance(self.n, int) or 0 <= self.head(q) < HEADS

    def tiles(self):
        return [s for s in range(QUAD) if self.exists(s)]

    def columns(self):
        tiles = self.tiles()
        return slice(tiles[0] * P, tiles[-1] * P + P)

    def uses(self, q, ring):
        missing = len([m for m in range(QUAD - FIRST) if m % ring == q % ring])
        return self.n * (QUAD // ring) + (q // ring - missing)

    def stages(self, t):
        begun = not isinstance(self.n, int) or self.n > 0 or t >= START
        return [stage for stage in SLOTS[t] if begun and self.exists(stage[1])]


def static_group(n):
    return Group(n, n // 2, n % 2)


def wait(eng, sem, count):
    if not isinstance(count, int) or count > 0:
        eng.wait_ge(sem, count)


def flamingo_block(nc, x, ctx, g_xattn, g_ffn, taps, skip, gu_packed, gu_scales, dn_packed, dn_scales,
                   identity, out):
    with ExitStack() as es:
        def sb(name, shape, dt):
            return es.enter_context(nc.sbuf_tensor(name, shape, dt))

        def ps(name, shape, dt=F32):
            return es.enter_context(nc.psum_tensor(name, shape, dt))

        def sem(name):
            return es.enter_context(nc.semaphore(name))

        toeplitz = nc.dram_tensor("toeplitz_taps", [HEADS, 2, P + L], F16, kind="Internal").ap()
        tap_scale = nc.dram_tensor("tap_scale", [HEADS + QUAD, 1], F32, kind="Internal").ap()

        w_gu = sb("w_gu", [P, 2, LB, 2 * INNER], F16)
        w_dn = sb("w_dn", [P, 2, IC, L], F16)
        ident = sb("ident", [P, P], F32)
        ident16 = sb("ident16", [P, 2, P], F16)
        x_in = sb("x_in", [P, 4, L], F32)
        c_in = sb("c_in", [P, 2, L], F32)
        t_in = sb("t_in", [P, 2, 2, L], F16)
        c_scaled = sb("c_scaled", [P, L], F32)
        q_rows = sb("q_rows", [P, L], F32)
        c_cols = sb("c_cols", [P, LB * 2, EXT], F32)
        q_cols = sb("q_cols", [P, 2, LB * 2, EXT], F32)
        pair32 = sb("pair32", [P, LB * 2, PAIRS], F32)
        pair_hi = sb("pair_hi", [P, 2, LB * 2, PAIRS], F16)
        pair_lo = sb("pair_lo", [P, 2, LB * 2, PAIRS], F16)
        z = sb("z", [P, 2, 8, ZW], F32)
        z1 = sb("z1", [P, 2, 4, HALF], F32)
        z2 = sb("z2", [P, 2, 2, HALF], F32)
        z_wrap = sb("z_wrap", [P, 2, 24], F32)
        o_cols = sb("o_cols", [P, 2, LB, P], F32)
        bn = sb("bn", [P, 2, 6], F32)
        head_small = sb("head_small", [P, 4, 17], F32)
        tap_factor = sb("tap_factor", [P, 2, QUAD], F32)
        x1 = sb("x1", [P, 2, QUAD, L], F32)
        xn_rows = sb("xn_rows", [P, L], F32)
        xn_cols = sb("xn_cols", [P, 2, 2, LB, ROWS], F16)
        silu_g = sb("silu_g", [P, 2, ROWS], F32)
        h32 = sb("h32", [P, 2, ROWS], F32)
        h = sb("h", [P, 2, IC, ROWS], F16)
        square = sb("square", [P, 2, L], F32)
        tile_small = sb("tile_small", [P, 2, 4], F32)
        const = sb("const", [P, 24], F32)
        k_small = sb("k_small", [HEADS, 8], F32)
        scales = sb("scales", [P, (GU + IC) * LB], F16)
        scale_parts = sb("scale_parts", [P, 4, (GU + IC) * LB], F32)
        kp = silu_g[0:HEADS].rearrange("p a s -> p (a s)")[:, 0:P + L]
        kp_split = h32[0:HEADS].rearrange("p a s -> p (a s)")[:, 0:P + L].bitcast(F16).rearrange(
            "p (a s) -> p a s", a=2)
        packed_gu = x1[:, 1].rearrange("p q l -> p (q l)").bitcast(I32)[:, 0:GU * LB * WORDS]
        packed_dn = square[:, :, :].rearrange("p a l -> p (a l)").bitcast(I32)[:, 0:LB * IC * WORDS]
        VW = 6 * LB * WORDS
        h_words = h[:, :, :, :].rearrange("p a c s -> p (a c s)").bitcast(I32)
        unpacked = [h_words[:, n * 4 * VW:(n + 1) * 4 * VW] for n in range(3)]
        diag = h_words[:, 12 * VW:12 * VW + 2 * 2 * 4 * P // 2].bitcast(F16).rearrange(
            "p (w s j o) -> p w s j o", w=2, s=2, j=4)
        x_words = xn_cols[:, 1].rearrange("p a c s -> p (a c s)").bitcast(I32)
        signs = [x_words[:, n * VW:(n + 1) * VW] for n in range(2)]
        sizes = [x_words[:, (n + 2) * VW:(n + 3) * VW] for n in range(2)]

        PEAK, CPOW, CREC, MEAN, VAR, VE, RS, QS, QB, RF, MEAN2, VAR2, VE2, RS2, QB2, NEG, NEG2 = range(17)
        (MINUS_HALF, TANH_X, TANH_F, MAX_W, MAX_D, PEAK_W, PEAK_D, POW_W, POW_D, REC_W, REC_D, NORM_W, NORM_D,
         GATE_S, H_S, INV, INV2, EPS3) = range(18)

        def col(n):
            return const[:, n:n + 1]

        pair_bank = [[ps("gate0", [P, ROWS]), ps("up0", [P, ROWS])], [ps("gate1", [P, ROWS]), ps("up1", [P, ROWS])]]
        y_bank = pair_bank[1]
        conv_bank = ps("conv", [P, 2, 512])
        turn_a = ps("turn_a", [P, 512])
        turn_b = ps("turn_b", [P, 512])

        small_in, k_loaded, w_loaded, scales_in = sem("small_in"), sem("k_loaded"), sem("w_loaded"), sem("scales_in")
        x_loaded = [sem(f"x_loaded{n}") for n in range(4)]
        c_loaded = [sem(f"c_loaded{n}") for n in range(2)]
        t_loaded = [sem(f"t_loaded{n}") for n in range(2)]
        factor_loaded = [sem(f"factor_loaded{n}") for n in range(2)]
        taps_stored, factors_stored, ident_in = sem("taps_stored"), sem("factors_stored"), sem("ident_in")
        stored = [sem(f"stored{n}") for n in range(2)]
        zeroed, k_step, w_small, w_peak, tanh_done, ident_cast = (
            sem("zeroed"), sem("k_step"), sem("w_small"), sem("w_peak"), sem("tanh_done"), sem("ident_cast"))
        bits_done, unpack_done, diagonals_made, w_turned, w_taken, scales_split = (
            sem("bits_done"), sem("unpack_done"), sem("diagonals_made"), sem("w_turned"), sem("w_taken"),
            sem("scales_split"))
        c_peak, x_moments, c_clamped, x_aggr, c_pow, var_ready, c_recip = (
            sem("c_peak"), sem("x_moments"), sem("c_clamped"), sem("x_aggr"), sem("c_pow"), sem("var_ready"),
            sem("c_recip"))
        rs_ready, q_scale, q_affine, row_factor = sem("rs_ready"), sem("q_scale"), sem("q_affine"), sem("row_factor")
        c_rows_ready, q_rows_ready, c_turned, q_turned = (
            sem("c_rows_ready"), sem("q_rows_ready"), sem("c_turned"), sem("q_turned"))
        c_cols_ready, q_cols_ready, pairs_ready, pairs_hi, pairs_lo = (
            sem("c_cols_ready"), sem("q_cols_ready"), sem("pairs_ready"), sem("pairs_hi"), sem("pairs_lo"))
        conv_done, z_filled, z1_done, z2_done, wrap_done, o_summed, o_ready = (
            sem("conv_done"), sem("z_filled"), sem("z1_done"), sem("z2_done"), sem("wrap_done"), sem("o_summed"),
            sem("o_ready"))
        out_turned, x1_ready, x1_moments, x1_aggr, var2_ready, rs2_ready, xn_affine = (
            sem("out_turned"), sem("x1_ready"), sem("x1_moments"), sem("x1_aggr"), sem("var2_ready"),
            sem("rs2_ready"), sem("xn_affine"))
        xn_rows_ready, xn_turned, xn_hi, xn_lo = (
            sem("xn_rows_ready"), sem("xn_turned"), sem("xn_hi"), sem("xn_lo"))
        gate_done, up_done, silu_done, h_ready, h_hi, h_lo = (
            sem("gate_done"), sem("up_done"), sem("silu_done"), sem("h_ready"), sem("h_hi"), sem("h_lo"))
        y_done, squared, mean_square, y_rs, y_scale, out_ready = (
            sem("y_done"), sem("squared"), sem("mean_square"), sem("y_rs"), sem("y_scale"), sem("out_ready"))

        def small(q, c, n=1):
            return head_small[:, q % 4, c:c + n]

        def spread(ap, step, count):
            a = [list(pair) for pair in ap.ap]
            return bass.AP(tensor=ap.tensor, offset=ap.offset, ap=[a[0], a[1], [step, count], a[2]])

        def pairs(eng, grp, q, n):
            if n == 0:
                wait(eng, pairs_hi, grp.head(q) * 2)
                wait(eng, pairs_lo, grp.head(q) * 2)
                eng.wait_ge(c_cols_ready, grp.head(q) * 2 + 2)
            g = slice(4 * n, 4 * n + 4)
            first = c_cols[:, g, 0:HALF]
            eng.tensor_tensor(pair32[:, g, 0:4 * HALF].rearrange("p g (d c) -> p g d c", d=4),
                              spread(first, 0, 4), spread(first, 8, 4), ALU.mult).then_inc(pairs_ready, 1)
            eng.tensor_tensor(pair32[:, g, 4 * HALF:PAIRS], c_cols[:, g, 0:32], c_cols[:, g, 32:64],
                              ALU.mult).then_inc(pairs_ready, 1)

        def pairs_low(eng, grp, q, n):
            eng.wait_ge(pairs_hi, grp.head(q) * 2 + n + 1)
            g = slice(4 * n, 4 * n + 4)
            eng.tensor_tensor(pair_lo[:, q % 2, g, :], pair32[:, g, :], pair_hi[:, q % 2, g, :],
                              ALU.subtract).then_inc(pairs_lo, 1)

        def diagonals(eng, w, part):
            _, is_down, tile, c0, count = PIECES[w]
            c = GU * LB + tile * IC + c0 if is_down else tile * LB
            one, factor = ident16[:, is_down, :], scale_parts[:, part, c:c + count]
            return eng.tensor_tensor(diag[:, w % 2, part, 0:count, :],
                                     bass.AP(tensor=one.tensor, offset=one.offset,
                                             ap=[list(one.ap[0]), [0, count], list(one.ap[1])]),
                                     bass.AP(tensor=factor.tensor, offset=factor.offset,
                                             ap=[list(factor.ap[0]), list(factor.ap[1]), [0, P]]), ALU.mult)

        PAIRED = (GROUPS - 3) // 2

        def run_groups(eng, group_program):
            group_program(static_group(0))
            group_program(static_group(1))
            with eng.Fori(0, PAIRED) as turn:
                group_program(Group(turn * 2 + 2, turn + 1, 0))
                group_program(Group(turn * 2 + 3, turn + 1, 1))
            group_program(static_group(GROUPS - 1))
            group_program(static_group(GROUPS))

        def feeds(grp):
            return grp.prev().tiles() if not isinstance(grp.n, int) or grp.n > 0 else []

        block = es.enter_context(nc.Block())

        @block.sync
        def _(sp):
            def rows_of(tensor, grp, q, half):
                if isinstance(grp.n, int):
                    channels = slice(grp.head(q) * HD, grp.head(q) * HD + HD)
                else:
                    channels = bass.ds(grp.n * (QUAD * HD) + (q - (QUAD - FIRST)) * HD, HD)
                return tensor[8 * half:8 * half + 8, channels, :].rearrange("b i l -> i b l")

            def load_c(grp, q):
                wait(sp, c_rows_ready, grp.head(q) - 1)
                for half in range(2):
                    sp.dma_start(c_in[64 * half:64 * half + 64, q % 2, :],
                                 rows_of(ctx, grp, q, half)).then_inc(c_loaded[q % 2], 16)

            def load_x(grp, q):
                wait(sp, x1_ready, grp.head(q) - 3)
                for half in range(2):
                    sp.dma_start(x_in[64 * half:64 * half + 64, q % 4, :],
                                 rows_of(x, grp, q, half)).then_inc(x_loaded[q % 4], 16)

            def load_taps(grp, q):
                wait(sp, conv_done, grp.head(q) * LB - LB)
                if isinstance(grp.n, int):
                    first = toeplitz[grp.head(q):grp.head(q) + 1, 0, 1:1 + L]
                else:
                    first = toeplitz[bass.ds(grp.head(q), 1), 0, 1:1 + L]
                windows = bass.AP(tensor=first.tensor, offset=first.offset, ap=[[1, P], [P + L, 2], [1, L]])
                sp.dma_start(t_in[:, q % 2, :, :], windows).then_inc(t_loaded[q % 2], 16)

            def load_factor(grp):
                skipped = grp.tiles()[0]
                if isinstance(grp.n, int):
                    first = tap_scale[grp.head(skipped):grp.head(QUAD), 0:1]
                else:
                    first = tap_scale[bass.ds(grp.head(0), QUAD), 0:1]
                everywhere = bass.AP(tensor=first.tensor, offset=first.offset, ap=[[0, P], [1, QUAD - skipped]])
                sp.dma_start(tap_factor[:, grp.parity, skipped:], everywhere).then_inc(factor_loaded[grp.parity], 16)

            def store(grp, q):
                sp.wait_ge(out_ready, grp.head(q) + 1)
                for half in range(2):
                    sp.dma_start(rows_of(out, grp, q, half),
                                 x1[64 * half:64 * half + 64, grp.parity, q, :]).then_inc(stored[grp.parity], 16)

            def one_group(grp):
                tiles = feeds(grp)
                for t in range(UNITS + 3):
                    for stage, q, *_n in grp.stages(t):
                        if stage == "load_ct":
                            if grp.exists(q + 1):
                                load_taps(grp, q + 1)
                            if grp.exists(q + 2):
                                load_c(grp, q + 2)
                        elif stage == "load_x":
                            if grp.exists(q + 2):
                                load_x(grp, q + 2)
                            if q == 1 and grp.exists(QUAD):
                                load_factor(grp.next())
                    if t >= 27 and (t - 27) % 3 == 0 and (t - 27) // 3 < len(tiles):
                        store(grp.prev(), tiles[(t - 27) // 3])

            sp.wait_ge(zeroed, 1)
            sp.dma_start(kp[:, P:], taps).then_inc(k_loaded, 16)
            sp.dma_start(k_small[:, 0:1], skip).then_inc(k_loaded, 16)
            first = static_group(0)
            load_c(first, FIRST)
            load_x(first, FIRST)
            sp.dma_start(const[:, TANH_X:TANH_X + 1], g_xattn.partition_broadcast(P)).then_inc(small_in, 16)
            sp.dma_start(const[:, TANH_F:TANH_F + 1], g_ffn.partition_broadcast(P)).then_inc(small_in, 16)
            sp.dma_start(ident[:, :], identity).then_inc(ident_in, 16)
            sp.dma_start(scales[:, 0:GU * LB], gu_scales).then_inc(scales_in, 16)
            sp.dma_start(scales[:, GU * LB:], dn_scales).then_inc(scales_in, 16)
            sp.wait_ge(k_step, 6)
            sp.dma_start(toeplitz, kp_split[:, :, :]).then_inc(taps_stored, 16)
            sp.dma_start(packed_gu, gu_packed).then_inc(w_loaded, 16)
            sp.dma_start(packed_dn, dn_packed).then_inc(w_loaded, 16)
            sp.wait_ge(taps_stored, 16)
            load_taps(first, FIRST)
            load_c(first, FIRST + 1)
            load_x(first, FIRST + 1)
            sp.wait_ge(k_step, 7)
            sp.dma_start(tap_scale[0:HEADS], k_small[:, 3:4]).then_inc(factors_stored, 16)
            sp.dma_start(tap_scale[HEADS:], k_small[0:QUAD, 3:4]).then_inc(factors_stored, 16)
            sp.wait_ge(factors_stored, 32)
            load_factor(first)
            load_factor(first.next())
            run_groups(sp, one_group)
            for n in range(2):
                sp.wait_ge(stored[n], 2 * 16 * HEADS // 2)

        @block.tensor
        def _(pe):
            def turn(bank, src, done):
                for b in range(LB):
                    mm = pe.transpose(bank[:, P * b:P * b + P], src[:, b], ident[:, :])
                mm.then_inc(done, 1)

            def turned_out_before(grp, q):
                return grp.head(q) - (1 if q == 1 else 2)

            def turned_in_before(grp, q):
                heads = grp.head(q + (3 if q < QUAD - 1 else 2))
                return min(heads, HEADS) if isinstance(heads, int) else heads

            def turn_c(grp, q):
                wait(pe, c_cols_ready, grp.head(q) * 2)
                wait(pe, x1_ready, turned_out_before(grp, q))
                pe.wait_ge(c_rows_ready, grp.head(q) + 1)
                turn(turn_a, c_scaled[:, :].rearrange("p (b t) -> p b t", b=LB), c_turned)

            def turn_q(grp, q):
                wait(pe, q_cols_ready, grp.head(q) * 2)
                wait(pe, xn_lo, turned_out_before(grp, q))
                pe.wait_ge(q_rows_ready, grp.head(q) + 1)
                turn(turn_b, q_rows[:, :].rearrange("p (b t) -> p b t", b=LB), q_turned)

            def turn_out(grp, q):
                pe.wait_ge(c_cols_ready, turned_in_before(grp, q) * 2)
                wait(pe, x1_ready, grp.head(q))
                pe.wait_ge(o_ready, (grp.head(q) + 1) * LB)
                turn(turn_a, o_cols[:, q % 2], out_turned)

            def turn_x(grp, q):
                pe.wait_ge(q_cols_ready, turned_in_before(grp, q) * 2)
                wait(pe, xn_lo, grp.head(q))
                pe.wait_ge(xn_rows_ready, grp.head(q) + 1)
                turn(turn_b, xn_rows[:, :].rearrange("p (b t) -> p b t", b=LB), xn_turned)

            def conv(grp, q, n):
                wait(pe, z_filled, (grp.head(q) * LB + n) * 3)
                if n == 0:
                    pe.wait_ge(t_loaded[q % 2], (grp.uses(q, 2) + 1) * 16)
                if n % 2 == 0:
                    pe.wait_ge(pairs_lo, grp.head(q) * 2 + n // 2 + 1)
                for b in range(n + 1):
                    for part, moving in ((0, (pair_hi, pair_lo)), (1, (pair_hi,))):
                        w = t_in[:, q % 2, part, (n - b) * P:(n - b + 1) * P]
                        for m in moving:
                            for half in range(2):
                                mm = pe.matmul(conv_bank[:, half, 0:PAIRS], w, m[:, q % 2, 2 * b + half, :],
                                               start=(b == 0 and part == 0 and m is pair_hi),
                                               stop=(b == n and part == 1))
                mm.then_inc(conv_done, 1)

            def products(bank, steps):
                for k, (sta, mov) in enumerate(steps):
                    pe.matmul(bank, sta(0), mov(0), start=(k == 0), stop=False)
                    pe.matmul(bank, sta(0), mov(1), start=False, stop=False)
                    mm = pe.matmul(bank, sta(1), mov(0), start=False, stop=(k == len(steps) - 1))
                return mm

            def gate_or_up(grp, u, up):
                f = grp.n * IC
                tiles = grp.tiles()
                if u == 0 and not up:
                    pe.wait_ge(xn_lo, grp.head(tiles[-1]) + 1)
                if u == 1:
                    wait(pe, out_ready, grp.head(tiles[0]))
                elif u > 1 and up:
                    pe.wait_ge(h_ready, f + u - 1)
                elif u > 1:
                    pe.wait_ge(silu_done, f + u - 1)
                o = (IC * up + u) * P
                steps = [(lambda part, b=b: w_gu[:, part, b, o:o + P],
                          lambda part, b=b: xn_cols[:, grp.parity, part, b, grp.columns()]) for b in range(LB)]
                products(pair_bank[u % 2][up][:, grp.columns()], steps).then_inc(up_done if up else gate_done, 1)

            def down(grp, s, part):
                f = grp.n * IC
                place = grp.tiles().index(s)
                if part == 0:
                    if place == 0:
                        pe.wait_ge(silu_done, f + IC - 1)
                    elif place == 1:
                        pe.wait_ge(h_ready, f + IC - 1)
                    else:
                        pe.wait_ge(out_ready, grp.head(s) - 1)
                for c in DOWN_PARTS[part]:
                    if place == 0:
                        pe.wait_ge(h_lo, f + c + 1)
                    bank = y_bank[s % 2][:, :]
                    rows = slice(s * P, s * P + P)
                    pe.matmul(bank, h[:, 0, c, rows], w_dn[:, 0, c, :], start=(c == 0), stop=False)
                    pe.matmul(bank, h[:, 0, c, rows], w_dn[:, 1, c, :], start=False, stop=False)
                    mm = pe.matmul(bank, h[:, 1, c, rows], w_dn[:, 0, c, :], start=False, stop=(c == IC - 1))
                if part == 2:
                    mm.then_inc(y_done, 1)

            def weights(w):
                batch, is_down, tile, c0, count = PIECES[w]
                if w >= 2:
                    pe.wait_ge(w_taken, 2 * (w - 1))
                pe.wait_ge(unpack_done, batch + 1)
                values = unpacked[batch % 3].bitcast(F16)
                for part in range(2):
                    pe.wait_ge(diagonals_made, 2 * w + part + 1)
                    for j in range(count):
                        c = (tile - BATCHES[batch][1]) * (IC if is_down else LB) + c0 + j
                        mm = pe.matmul(pair_bank[w % 2][part][:, P * j:P * j + P], values[:, P * c:P * c + P],
                                       diag[:, w % 2, part, j, :], start=True, stop=True)
                    mm.then_inc(w_turned, 1)

            def one_group(grp):
                tiles = feeds(grp)
                for t in range(UNITS):
                    for stage, q, *n in grp.stages(t):
                        if stage == "conv":
                            conv(grp, q, n[0])
                        elif stage == "turn_c":
                            turn_c(grp, q)
                        elif stage == "turn_q":
                            turn_q(grp, q)
                        elif stage == "turn_out":
                            turn_out(grp, q)
                        elif stage == "turn_x":
                            turn_x(grp, q)
                    if tiles and t < 2 * IC:
                        gate_or_up(grp.prev(), t // 2, t % 2)
                    elif tiles and (t - 2 * IC) // 3 < len(tiles):
                        down(grp.prev(), tiles[(t - 2 * IC) // 3], (t - 2 * IC) % 3)
                    elif not tiles:
                        for w in pieces_at(t):
                            weights(w)
                if not tiles:
                    pe.wait_ge(w_taken, 2 * len(PIECES))

            pe.wait_ge(ident_in, 16)
            run_groups(pe, one_group)

        @block.scalar
        def _(act):
            def scale_c(grp, q):
                wait(act, c_turned, grp.head(q))
                act.wait_ge(c_recip, grp.head(q) + 1)
                act.activation(c_scaled[:, :].rearrange("p (b t) -> p b t", b=LB)[:, :, ::-1],
                               c_in[:, q % 2, :].rearrange("p (b t) -> p b t", b=LB),
                               ACT.Copy, scale=small(q, CREC)).then_inc(c_rows_ready, 1)

            def make_q(grp, q):
                wait(act, q_turned, grp.head(q))
                act.wait_ge(q_affine, grp.head(q) + 1)
                act.activation(q_rows[:, :], x_in[:, q % 4, :], ACT.Identity, scale=small(q, QS),
                               bias=small(q, QB)).then_inc(q_rows_ready, 1)

            def extend(dst, bank, done, scale):
                src = bank[:, :].rearrange("p (g c) -> p g c", c=HALF)
                act.activation(dst[:, :, 0:HALF], src, ACT.Copy, scale=scale).then_inc(done, 1)
                act.activation(dst[:, :, HALF:EXT], src[:, :, 0:EXT - HALF], ACT.Copy, scale=scale).then_inc(done, 1)

            def take_c(grp, q):
                wait(act, pairs_ready, grp.head(q) * 4)
                act.wait_ge(c_turned, grp.head(q) + 1)
                extend(c_cols, turn_a, c_cols_ready, 32.0)

            def take_q(grp, q):
                wait(act, z_filled, (grp.head(q) - 1) * LB * 3)
                act.wait_ge(q_turned, grp.head(q) + 1)
                extend(q_cols[:, q % 2], turn_b, q_cols_ready, 1.0)

            def pairs_high(grp, q, n):
                if n == 0:
                    wait(act, conv_done, (grp.head(q) - 1) * LB)
                act.wait_ge(pairs_ready, grp.head(q) * 4 + 2 * n + 2)
                act.activation(pair_hi[:, q % 2, 4 * n:4 * n + 4, :], pair32[:, 4 * n:4 * n + 4, :],
                               ACT.Copy).then_inc(pairs_hi, 1)

            def normalise(grp, q):
                wait(act, xn_turned, grp.head(q))
                act.wait_ge(xn_affine, grp.head(q) + 1)
                act.activation(xn_rows[:, :].rearrange("p (b k m) -> p b m k", b=LB, k=4),
                               x1[:, grp.parity, q, :].rearrange("p (b m k) -> p b m k", b=LB, k=4),
                               ACT.Identity, scale=small(q, RS2),
                               bias=small(q, QB2)).then_inc(xn_rows_ready, 1)

            def x_high(grp, q):
                act.wait_ge(xn_turned, grp.head(q) + 1)
                act.activation(xn_cols[:, grp.parity, 0, :, q * P:q * P + P],
                               turn_b[:, :].rearrange("p (b r) -> p b r", b=LB), ACT.Copy).then_inc(xn_hi, 1)

            def silu(grp, u):
                f = grp.n * IC
                if u >= 2:
                    act.wait_ge(h_ready, f + u - 1)
                act.wait_ge(gate_done, f + u + 1)
                act.activation(silu_g[:, u % 2, grp.columns()], pair_bank[u % 2][0][:, grp.columns()], ACT.Silu,
                               scale=col(GATE_S)).then_inc(silu_done, 1)

            def h_high(grp, u):
                f = grp.n * IC
                act.wait_ge(h_ready, f + u + 1)
                act.activation(h[:, 0, u, grp.columns()], h32[:, u % 2, grp.columns()], ACT.Copy).then_inc(h_hi, 1)

            def take_weights(w):
                _, is_down, tile, c0, count = PIECES[w]
                if w == 0:
                    act.wait_ge(w_small, 10)
                cols = slice(tile * P, tile * P + P)
                for part in range(2):
                    act.wait_ge(w_turned, 2 * w + part + 1)
                    dst = w_dn[:, part, c0:c0 + count, cols] if is_down else w_gu[:, part, :, cols]
                    act.activation(dst, pair_bank[w % 2][part][:, 0:count * P].rearrange("p (c o) -> p c o", o=P),
                                   ACT.Copy, scale=col(NORM_D if is_down else NORM_W)).then_inc(w_taken, 1)

            def square_y(grp, s):
                if grp.tiles().index(s) >= 2:
                    act.wait_ge(mean_square, grp.head(s) - 1)
                act.wait_ge(y_done, grp.head(s) + 1)
                act.activation(square[:, s % 2, :], y_bank[s % 2][:, :], ACT.Square,
                               scale=L ** -0.5, accum_out=tile_small[:, s % 2, 0:1]).then_inc(squared, 2)

            def one_group(grp):
                tiles = feeds(grp)
                for t in range(UNITS + 2):
                    if tiles:
                        if t % 2 == 1 and t < 2 * IC:
                            silu(grp.prev(), t // 2)
                        if t % 2 == 0 and 2 <= t <= 2 * IC:
                            h_high(grp.prev(), t // 2 - 1)
                        if t >= 25 and (t - 25) % 3 == 0 and (t - 25) // 3 < len(tiles):
                            square_y(grp.prev(), tiles[(t - 25) // 3])
                    for stage, q, *n in grp.stages(t):
                        if stage == "turn_c":
                            take_c(grp, q)
                        elif stage == "turn_q":
                            take_q(grp, q)
                        elif stage == "turn_x":
                            x_high(grp, q)
                    for w in pieces_at(t) if not tiles else ():
                        take_weights(w)
                    for stage, q, *n in grp.stages(t):
                        if stage == "pairs":
                            pairs_high(grp, q, n[0])
                        elif stage == "turn_out":
                            normalise(grp, q)
                        elif stage == "stats":
                            scale_c(grp, q)
                            make_q(grp, q)

            act.wait_ge(small_in, 32)
            act.activation(col(TANH_X), col(TANH_X), ACT.Tanh).then_inc(tanh_done, 1)
            act.activation(col(TANH_F), col(TANH_F), ACT.Tanh).then_inc(tanh_done, 1)
            first = static_group(0)
            scale_c(first, FIRST)
            make_q(first, FIRST)
            run_groups(act, one_group)

        @block.gpsimd
        def _(pool):
            def row_scalars(grp, q):
                n = grp.head(q)
                pool.wait_ge(var_ready, 2 * n + 2)
                pool.tensor_tensor(small(q, RS), small(q, VE), col(MINUS_HALF), ALU.pow).then_inc(rs_ready, 1)
                pool.wait_ge(c_recip, n + 1)
                pool.wait_ge(rs_ready, n + 1)
                pool.tensor_tensor(small(q, QS), small(q, RS), small(q, CPOW), ALU.mult).then_inc(q_scale, 1)
                pool.wait_ge(q_scale, n + 1)
                pool.tensor_tensor(small(q, QB), small(q, NEG), small(q, QS), ALU.mult).then_inc(q_affine, 1)
                if q == QUAD or isinstance(n, int) and n == 0:
                    home = grp.next() if q == QUAD else grp
                    pool.wait_ge(factor_loaded[home.parity], (home.halved + 1) * 16)
                parity = grp.parity if q < QUAD else 1 - grp.parity
                pool.tensor_tensor(small(q, RF), small(q, CPOW), tap_factor[:, parity, q % 4:q % 4 + 1],
                                   ALU.mult).then_inc(row_factor, 1)

            def norm_scalars(grp, q):
                n = grp.head(q)
                pool.wait_ge(var2_ready, 2 * n + 2)
                pool.tensor_tensor(small(q, RS2), small(q, VE2), col(MINUS_HALF), ALU.pow).then_inc(rs2_ready, 1)
                pool.wait_ge(rs2_ready, n + 1)
                pool.tensor_tensor(small(q, QB2), small(q, NEG2), small(q, RS2), ALU.mult).then_inc(xn_affine, 1)

            def y_scalars(grp, s):
                n = grp.head(s)
                pool.wait_ge(squared, 2 * n + 2)
                pool.tensor_tensor(tile_small[:, s % 2, 1:2], tile_small[:, s % 2, 0:1], col(EPS3),
                                   ALU.add).then_inc(mean_square, 1)
                pool.wait_ge(mean_square, n + 1)
                pool.tensor_tensor(tile_small[:, s % 2, 2:3], tile_small[:, s % 2, 1:2], col(MINUS_HALF),
                                   ALU.pow).then_inc(y_rs, 1)
                if grp.tiles().index(s) >= 2:
                    pool.wait_ge(out_ready, n - 1)
                pool.wait_ge(y_rs, n + 1)
                pool.tensor_tensor(tile_small[:, s % 2, 3:4], tile_small[:, s % 2, 2:3], col(TANH_F),
                                   ALU.mult).then_inc(y_scale, 1)

            def one_group(grp):
                tiles = feeds(grp)
                for t in range(UNITS + 2):
                    if t >= 25 and (t - 25) % 3 == 0 and (t - 25) // 3 < len(tiles):
                        y_scalars(grp.prev(), tiles[(t - 25) // 3])
                    for w in pieces_at(t) if not tiles else ():
                        if w >= 2:
                            pool.wait_ge(w_turned, 2 * (w - 1))
                        diagonals(pool, w, 0).then_inc(diagonals_made, 1)
                        diagonals(pool, w, 1).then_inc(diagonals_made, 1)
                    for stage, q, *n in grp.stages(t):
                        if stage == "stats":
                            row_scalars(grp, q)
                        elif stage == "pairs" and tiles:
                            pairs(pool, grp, q, n[0])
                        elif stage == "conv" and tiles and n[0] == 2 and grp.exists(q + 1):
                            pairs_low(pool, grp, q + 1, 0)
                            pairs_low(pool, grp, q + 1, 1)
                        elif stage == "turn_out":
                            norm_scalars(grp, q)

            pool.wait_ge(w_small, 2)
            pool.partition_all_reduce(col(PEAK_W), col(MAX_W), P, RMAX).then_inc(w_peak, 1)
            pool.partition_all_reduce(col(PEAK_D), col(MAX_D), P, RMAX).then_inc(w_peak, 1)
            first = static_group(0)
            row_scalars(first, FIRST)
            pool.wait_ge(ident_cast, 2)
            pool.wait_ge(scales_split, 4)
            run_groups(pool, one_group)

        @block.vector
        def _(dve):
            def stats(grp, q):
                n = grp.head(q)
                dve.wait_ge(c_loaded[q % 2], (grp.uses(q, 2) + 1) * 32)
                dve.tensor_reduce(small(q, PEAK), c_in[:, q % 2, :], AX_X, ALU.max,
                                  apply_absolute_value=True).then_inc(c_peak, 1)
                dve.wait_ge(x_loaded[q % 4], (grp.uses(q, 4) + 1) * 32)
                dve.bn_stats(bn[:, 0, :], x_in[:, q % 4, :]).then_inc(x_moments, 1)
                dve.wait_ge(x_moments, n + 1)
                dve.wait_ge(c_peak, n + 1)
                dve.tensor_scalar(small(q, PEAK), small(q, PEAK), 2.0 ** -60, None, ALU.max).then_inc(c_clamped, 1)
                dve.bn_aggr(small(q, MEAN, 2), bn[:, 0, :]).then_inc(x_aggr, 1)
                dve.wait_ge(c_clamped, n + 1)
                dve.tensor_scalar(small(q, CPOW).bitcast(I32), small(q, PEAK).bitcast(I32), 0x7F800000, None,
                                  ALU.bitwise_and).then_inc(c_pow, 1)
                dve.wait_ge(x_aggr, n + 1)
                dve.tensor_scalar(small(q, NEG), small(q, MEAN), -1.0, None, ALU.mult).then_inc(var_ready, 1)
                dve.tensor_scalar(small(q, VE), small(q, VAR), LN_EPS, 1024.0, ALU.add, ALU.mult).then_inc(var_ready, 1)
                dve.wait_ge(c_pow, n + 1)
                dve.reciprocal(small(q, CREC), small(q, CPOW)).then_inc(c_recip, 1)

            def weigh(grp, q, n):
                m = grp.head(q) * LB + n
                if n == 0:
                    dve.wait_ge(q_cols_ready, grp.head(q) * 2 + 2)
                    wait(dve, out_turned, grp.head(q) - 1)
                wait(dve, z1_done, m)
                wait(dve, wrap_done, m)
                dve.wait_ge(conv_done, m + 1)
                y = conv_bank[:, :, 0:HALF]
                ql = q_cols[:, q % 2, 2 * n:2 * n + 2, 0:HALF]
                dve.tensor_tensor(spread(z[:, :, 0, 0:HALF], ZW + 8, 4), spread(y, HALF, 4), spread(ql, 0, 4),
                                  ALU.mult).then_inc(z_filled, 1)
                dve.tensor_tensor(z[:, :, 4:7, 0:HALF], spread(conv_bank[:, :, HALF:2 * HALF], HALF, 3),
                                  spread(q_cols[:, q % 2, 2 * n:2 * n + 2, 8:8 + HALF], 8, 3),
                                  ALU.mult).then_inc(z_filled, 1)
                dve.tensor_tensor(z[:, :, 7, 0:HALF].rearrange("p g (k c) -> p g k c", k=2),
                                  spread(conv_bank[:, :, 4 * HALF:PAIRS], 0, 2),
                                  spread(q_cols[:, q % 2, 2 * n:2 * n + 2, 32:64], 32, 2),
                                  ALU.mult).then_inc(z_filled, 1)
                dve.wait_ge(z_filled, 3 * m + 3)
                wait(dve, z2_done, m)
                dve.tensor_tensor(z1[:, :, :, :], z[:, :, 0:4, 0:HALF], z[:, :, 4:8, 0:HALF],
                                  ALU.add).then_inc(z1_done, 1)
                wait(dve, o_ready, m)
                dve.tensor_reduce(z_wrap[:, :, :], z[:, :, 1:4, HALF:HALF + 24].rearrange("p g d c -> p g c d"), AX_X,
                                  ALU.add).then_inc(wrap_done, 1)
                dve.wait_ge(z1_done, m + 1)
                dve.tensor_tensor(z2[:, :, :, :], z1[:, :, 0:2, :], z1[:, :, 2:4, :], ALU.add).then_inc(z2_done, 1)
                dve.wait_ge(z2_done, m + 1)
                o = o_cols[:, q % 2, n, :].rearrange("p (g c) -> p g c", g=2)
                dve.tensor_tensor(o, z2[:, :, 0, :], z2[:, :, 1, :], ALU.add).then_inc(o_summed, 1)
                dve.wait_ge(wrap_done, m + 1)
                dve.wait_ge(o_summed, m + 1)
                dve.tensor_tensor(o[:, :, 0:24], o[:, :, 0:24], z_wrap[:, :, :], ALU.add).then_inc(o_ready, 1)

            def add_attention(grp, q):
                n = grp.head(q)
                if q == grp.tiles()[0]:
                    wait(dve, stored[grp.parity], (grp.halved * QUAD - (QUAD - FIRST) * (1 - grp.parity)) * 2 * 16)
                dve.wait_ge(row_factor, n + 1)
                dve.wait_ge(out_turned, n + 1)
                dve.scalar_tensor_tensor(x1[:, grp.parity, q, :], turn_a[:, :], small(q, RF), x_in[:, q % 4, :],
                                         ALU.mult, ALU.add).then_inc(x1_ready, 1)
                dve.wait_ge(x1_ready, n + 1)
                dve.bn_stats(bn[:, 1, :], x1[:, grp.parity, q, :]).then_inc(x1_moments, 1)
                dve.wait_ge(x1_moments, n + 1)
                dve.tensor_copy(small(q, VE2), small(q, VE2))
                dve.bn_aggr(small(q, MEAN2, 2), bn[:, 1, :]).then_inc(x1_aggr, 1)
                dve.wait_ge(x1_aggr, n + 1)
                dve.tensor_scalar(small(q, NEG2), small(q, MEAN2), -1.0, None, ALU.mult).then_inc(var2_ready, 1)
                dve.tensor_scalar(small(q, VE2), small(q, VAR2), LN_EPS, 2.0 ** -16, ALU.add,
                                  ALU.mult).then_inc(var2_ready, 1)

            def x_low(grp, q):
                dve.wait_ge(xn_hi, grp.head(q) + 1)
                dve.tensor_tensor(xn_cols[:, grp.parity, 1, :, q * P:q * P + P],
                                  turn_b[:, :].rearrange("p (b r) -> p b r", b=LB),
                                  xn_cols[:, grp.parity, 0, :, q * P:q * P + P], ALU.subtract).then_inc(xn_lo, 1)

            def make_h(grp, u):
                f = grp.n * IC
                if u >= 2:
                    dve.wait_ge(h_hi, f + u - 1)
                dve.wait_ge(up_done, f + u + 1)
                dve.wait_ge(silu_done, f + u + 1)
                cols = grp.columns()
                dve.scalar_tensor_tensor(h32[:, u % 2, cols], pair_bank[u % 2][1][:, cols], col(H_S), silu_g[:, u % 2, cols],
                                         ALU.mult, ALU.mult).then_inc(h_ready, 1)

            def h_low(grp, u):
                dve.wait_ge(h_hi, grp.n * IC + u + 1)
                cols = grp.columns()
                dve.tensor_tensor(h[:, 1, u, cols], h32[:, u % 2, cols], h[:, 0, u, cols], ALU.subtract).then_inc(h_lo, 1)

            def finish(grp, s):
                dve.wait_ge(y_scale, grp.head(s) + 1)
                rows = x1[:, grp.parity, s, :]
                dve.scalar_tensor_tensor(rows, y_bank[s % 2][:, :], tile_small[:, s % 2, 3:4], rows, ALU.mult,
                                         ALU.add).then_inc(out_ready, 1)

            bits = [2]

            def unpack(batch):
                is_down, t0, nt = BATCHES[batch]
                per_tile = (IC if is_down else LB) * WORDS
                n = nt * per_tile
                words = (packed_dn if is_down else packed_gu)[:, t0 * per_tile:t0 * per_tile + n]
                if batch >= 3:
                    done = 1 + max(w for w, piece in enumerate(PIECES) if piece[0] == batch - 3)
                    dve.wait_ge(w_turned, 2 * done)
                for k in range(4):
                    sign, size = signs[k % 2][:, 0:n], sizes[k % 2][:, 0:n]
                    shift = (ALU.logical_shift_left, 9 - 4 * k) if k < 3 else (ALU.logical_shift_right, 3)
                    dve.tensor_scalar(sign, words, 12 - 4 * k, -0x7FFF8000, ALU.logical_shift_left,
                                      ALU.bitwise_and).then_inc(bits_done, 1)
                    dve.tensor_scalar(size, words, shift[1], 0x0E000E00, shift[0], ALU.bitwise_and).then_inc(bits_done, 1)
                    bits[0] += 2
                    dve.wait_ge(bits_done, bits[0])
                    values = unpacked[batch % 3][:, 0:4 * n].rearrange("p (c k j) -> p c k j", k=4, j=WORDS)[:, :, k, :]
                    ins = dve.tensor_tensor(values, sign.rearrange("p (c j) -> p c j", j=WORDS),
                                            size.rearrange("p (c j) -> p c j", j=WORDS), ALU.bitwise_or)
                    ins.then_inc(bits_done, 1)
                    bits[0] += 1
                dve.wait_ge(bits_done, bits[0])
                dve.sem_inc(unpack_done, 1)

            def one_group(grp):
                tiles = feeds(grp)
                for t in range(UNITS + 2):
                    if tiles:
                        if t % 2 == 0 and 2 <= t <= 2 * IC:
                            make_h(grp.prev(), t // 2 - 1)
                        if t % 2 == 1 and 3 <= t <= 2 * IC + 1:
                            h_low(grp.prev(), (t - 3) // 2)
                        if t >= 26 and (t - 26) % 3 == 0 and (t - 26) // 3 < len(tiles):
                            finish(grp.prev(), tiles[(t - 26) // 3])
                    for w in pieces_at(t) if not tiles else ():
                        batch = PIECES[w][0]
                        if PIECES[w] == FIRST_PIECES[batch] and batch + 1 < len(BATCHES):
                            unpack(batch + 1)
                    for stage, q, *n in grp.stages(t):
                        if stage == "conv":
                            weigh(grp, q, n[0])
                        elif stage == "pairs" and not tiles:
                            pairs(dve, grp, q, n[0])
                        elif stage == "turn_out":
                            add_attention(grp, q)
                        elif stage == "turn_x":
                            x_low(grp, q)
                        elif stage == "stats":
                            if not tiles:
                                pairs_low(dve, grp, q - 1, 0)
                                pairs_low(dve, grp, q - 1, 1)
                            stats(grp, q)

            dve.memset(kp[:, 0:P], 0.0).then_inc(zeroed, 1)
            dve.memset(const[:, MINUS_HALF:MINUS_HALF + 1], -0.5).then_inc(zeroed, 1)
            dve.memset(z[:, :, :, :], 0.0).then_inc(zeroed, 1)
            dve.memset(head_small[:, :, :], 0.0).then_inc(zeroed, 1)
            dve.wait_ge(zeroed, 4)
            dve.wait_ge(k_loaded, 32)
            dve.tensor_tensor(kp[:, P:P + 1], kp[:, P:P + 1], k_small[:, 0:1], ALU.add).then_inc(k_step, 1)
            dve.wait_ge(k_step, 1)
            dve.tensor_reduce(k_small[:, 1:2], kp[:, P:], AX_X, ALU.max, apply_absolute_value=True).then_inc(k_step, 1)
            dve.wait_ge(k_step, 2)
            dve.tensor_scalar(k_small[:, 2:3], k_small[:, 1:2], 2.0 ** -60, None, ALU.max).then_inc(k_step, 1)
            dve.wait_ge(k_step, 3)
            dve.tensor_scalar(k_small[:, 4:5].bitcast(I32), k_small[:, 2:3].bitcast(I32), 0x7F800000, None,
                              ALU.bitwise_and).then_inc(k_step, 1)
            dve.wait_ge(k_step, 4)
            dve.reciprocal(k_small[:, 5:6], k_small[:, 4:5]).then_inc(k_step, 1)
            dve.wait_ge(k_step, 5)
            dve.tensor_scalar(kp[:, :], kp[:, :], k_small[:, 5:6], 32.0, ALU.mult, ALU.mult).then_inc(bits_done, 1)
            dve.wait_ge(bits_done, 1)
            dve.tensor_copy(kp_split[:, 0, :], kp[:, :]).then_inc(bits_done, 1)
            dve.wait_ge(bits_done, 2)
            dve.tensor_tensor(kp_split[:, 1, :], kp[:, :], kp_split[:, 0, :], ALU.subtract).then_inc(k_step, 1)
            dve.wait_ge(tanh_done, 2)
            dve.tensor_scalar(k_small[:, 3:4], k_small[:, 4:5], const[0:HEADS, TANH_X:TANH_X + 1], 2.0 ** -10, ALU.mult,
                              ALU.mult).then_inc(k_step, 1)

            dve.wait_ge(scales_in, 32)
            dve.tensor_reduce(col(MAX_W), scales[:, 0:GU * LB], AX_X, ALU.max, apply_absolute_value=True).then_inc(w_small, 1)
            dve.tensor_reduce(col(MAX_D), scales[:, GU * LB:], AX_X, ALU.max, apply_absolute_value=True).then_inc(w_small, 1)
            first = static_group(0)
            stats(first, FIRST)
            dve.wait_ge(ident_in, 16)
            dve.tensor_copy(ident16[:, 1, :], ident[:, :]).then_inc(ident_cast, 1)
            dve.tensor_copy(ident16[:, 0, :].rearrange("p (k m) -> p k m", k=4),
                            ident[:, :].rearrange("p (m k) -> p k m", k=4)).then_inc(ident_cast, 1)
            dve.wait_ge(w_peak, 2)
            peaks, powers, recips = (const[:, c:c + 2] for c in (PEAK_W, POW_W, REC_W))
            dve.tensor_scalar(peaks, peaks, 2.0 ** -24, None, ALU.max).then_inc(w_small, 1)
            dve.wait_ge(w_small, 3)
            dve.tensor_scalar(powers.bitcast(I32), peaks.bitcast(I32), 0x7F800000, None,
                              ALU.bitwise_and).then_inc(w_small, 1)
            dve.wait_ge(w_small, 4)
            dve.reciprocal(recips, powers).then_inc(w_small, 1)
            dve.tensor_scalar(col(GATE_S), col(POW_W), 2.0 ** -8, None, ALU.mult).then_inc(w_small, 1)
            dve.wait_ge(w_small, 6)
            dve.tensor_scalar(const[:, NORM_W:NORM_W + 2], recips, 2.0 ** 14, None, ALU.mult).then_inc(w_small, 1)
            dve.tensor_scalar(col(H_S), col(REC_W), 2.0 ** -18, None, ALU.mult).then_inc(w_small, 1)
            rest, hi, lo, scaled = (scale_parts[:, c, :] for c in (3, 0, 1, 2))
            dve.tensor_scalar(scaled, scales[:, :], 2.0 ** 15 + 1, None, ALU.mult).then_inc(scales_split, 1)
            dve.wait_ge(scales_split, 1)
            dve.tensor_tensor(rest, scaled, scales[:, :], ALU.subtract).then_inc(scales_split, 1)
            dve.wait_ge(scales_split, 2)
            dve.tensor_tensor(hi, scaled, rest, ALU.subtract).then_inc(scales_split, 1)
            dve.wait_ge(scales_split, 3)
            dve.tensor_tensor(lo, scales[:, :], hi, ALU.subtract).then_inc(scales_split, 1)
            dve.wait_ge(scales_split, 4)
            dve.tensor_scalar(col(INV), col(REC_W), col(REC_W), col(REC_D), ALU.mult, ALU.mult).then_inc(w_small, 1)
            dve.wait_ge(w_small, 9)
            dve.tensor_scalar(col(INV2), col(INV), 2.0 ** -10, None, ALU.mult).then_inc(w_small, 1)
            dve.wait_ge(w_small, 10)
            dve.tensor_scalar(col(EPS3), col(INV2), col(INV2), RMS_EPS, ALU.mult, ALU.mult).then_inc(w_small, 1)
            dve.wait_ge(w_small, 11)

            dve.wait_ge(w_loaded, 32)
            unpack(0)
            run_groups(dve, one_group)


def kernel(x, ctx_2048, g_xattn, g_ffn, L0_xattn_ssm_kernel, L0_xattn_D, L0_ffn_gate_up_packed, L0_ffn_gate_up_scales,
           L0_ffn_down_packed, L0_ffn_down_scales):
    import numpy as np
    import concourse.bacc as bacc
    from concourse.bass_utils import run_bass_kernel_spmd

    def packed_tiles(words):
        words = np.asarray(words)
        return np.ascontiguousarray(words.reshape(-1, P, words.shape[1]).transpose(1, 0, 2).reshape(P, -1))

    def scale_tiles(scales):
        scales = np.asarray(scales)
        return np.ascontiguousarray(scales.reshape(scales.shape[0], -1, P).transpose(2, 1, 0).reshape(P, -1))

    arrays = {
        "x": np.ascontiguousarray(x),
        "ctx": np.ascontiguousarray(ctx_2048),
        "g_xattn": np.ascontiguousarray(g_xattn),
        "g_ffn": np.ascontiguousarray(g_ffn),
        "taps": np.ascontiguousarray(L0_xattn_ssm_kernel),
        "skip": np.ascontiguousarray(L0_xattn_D).reshape(HEADS, 1),
        "gu_packed": packed_tiles(L0_ffn_gate_up_packed),
        "gu_scales": scale_tiles(L0_ffn_gate_up_scales),
        "dn_packed": packed_tiles(L0_ffn_down_packed),
        "dn_scales": scale_tiles(L0_ffn_down_scales),
        "identity": np.eye(P, dtype=np.float32),
    }
    nc = bacc.Bacc("TRN2", target_bir_lowering=False, num_devices=1)
    aps = [nc.dram_tensor(n, a.shape, mybir.dt.from_np(a.dtype), kind="ExternalInput").ap() for n, a in arrays.items()]
    out = nc.dram_tensor("out", (BATCH, CHANNELS, L), F32, kind="ExternalOutput").ap()
    flamingo_block(nc, *aps, out)
    result = run_bass_kernel_spmd(nc, [arrays], core_ids=[0])
    return result.results[0]["out"]
```

```python
from contextlib import ExitStack

import concourse.bass as bass
from concourse import mybir

F32 = mybir.dt.float32
F16 = mybir.dt.float16
I32 = mybir.dt.int32
ALU = mybir.AluOpType
ACT = mybir.ActivationFunctionType
AX_X = mybir.AxisListType.X
RMAX = bass.bass_isa.ReduceOp.max

P = 128
BATCH, CHANNELS, L = 16, 256, 512
HD = 8
HEADS = CHANNELS // HD
LB = L // P
QUAD = 4
FIRST = 2
LEAD = QUAD - FIRST
GROUPS = (HEADS - FIRST) // QUAD + 2
ROWS = QUAD * P
INNER = 1408
IC = INNER // P
GU = 2 * IC
HALF = HD * 8
EXT = HALF + 32
PAIRS = 4 * HALF + 32
ZW = 96
WORDS = 16
LN_EPS = 1e-5
RMS_EPS = 1e-6

UNITS = 2 * IC + 3 * QUAD
DOWN_PARTS = (range(0, 4), range(4, 8), range(8, IC))

SLOTS = [[] for _ in range(UNITS + 3)]
for _q in range(QUAD):
    _b = 7 * _q
    SLOTS[_b] += [("load_ct", _q), ("conv", _q, 0)]
    SLOTS[_b + 1] += [("load_x", _q), ("turn_c", _q + 1)]
    SLOTS[_b + 2] += [("conv", _q, 1), ("pairs", _q + 1, 0)]
    SLOTS[_b + 3] += [("turn_q", _q + 1), ("pairs", _q + 1, 1)]
    SLOTS[_b + 4] += [("conv", _q, 2)]
    SLOTS[_b + 5] += [("stats", _q + 2)]
    SLOTS[_b + 6] += [("conv", _q, 3)]
    if _q:
        SLOTS[_b + 3] += [("turn_out", _q - 1)]
        SLOTS[_b + 6] += [("turn_x", _q - 1)]
SLOTS[30] += [("turn_out", QUAD - 1)]
SLOTS[33] += [("turn_x", QUAD - 1)]

BATCHES = [(0, 0, 6), (0, 6, 6), (0, 12, 6), (0, 18, 4), (1, 0, 2), (1, 2, 2)]
PIECES = []
for _n, (_down, _t0, _nt) in enumerate(BATCHES):
    for _t in range(_t0, _t0 + _nt):
        for _c in range(0, IC if _down else LB, 4):
            PIECES.append((_n, _down, _t, _c, min(4, (IC if _down else LB) - _c)))


FIRST_PIECES = [next(piece for piece in PIECES if piece[0] == _n) for _n in range(len(BATCHES))]

START = 7 * LEAD - 6
PIECE_SLOTS = range(START + 2, UNITS - 3)


def pieces_at(t):
    if t not in PIECE_SLOTS:
        return ()
    n = t - PIECE_SLOTS[0]
    return range(n * len(PIECES) // len(PIECE_SLOTS), (n + 1) * len(PIECES) // len(PIECE_SLOTS))


class Group:

    def __init__(self, number, halved, parity):
        self.n, self.halved, self.parity = number, halved, parity

    def next(self):
        return Group(self.n + 1, self.halved + self.parity, 1 - self.parity)

    def prev(self):
        return Group(self.n - 1, self.halved - 1 + self.parity, 1 - self.parity)

    def head(self, q):
        return self.n * QUAD + (q - LEAD)

    def exists(self, q):
        return not isinstance(self.n, int) or 0 <= self.head(q) < HEADS

    def tiles(self):
        return [s for s in range(QUAD) if self.exists(s)]

    def columns(self):
        tiles = self.tiles()
        return slice(tiles[0] * P, tiles[-1] * P + P)

    def uses(self, q, ring):
        missing = len([m for m in range(LEAD) if m % ring == q % ring])
        return self.n * (QUAD // ring) + (q // ring - missing)

    def stages(self, t):
        begun = not isinstance(self.n, int) or self.n > 0 or t >= START
        return [stage for stage in SLOTS[t] if begun and self.exists(stage[1])]


def static_group(n):
    return Group(n, n // 2, n % 2)


def wait(eng, sem, count):
    if not isinstance(count, int) or count > 0:
        eng.wait_ge(sem, count)


def flamingo_block(nc, x, ctx, g_xattn, g_ffn, taps, skip, gu_packed, gu_scales, dn_packed, dn_scales,
                   identity, out):
    with ExitStack() as es:
        def sb(name, shape, dt):
            return es.enter_context(nc.sbuf_tensor(name, shape, dt))

        def ps(name, shape, dt=F32):
            return es.enter_context(nc.psum_tensor(name, shape, dt))

        def sem(name):
            return es.enter_context(nc.semaphore(name))

        toeplitz = nc.dram_tensor("toeplitz_taps", [HEADS, 2, P + L], F16, kind="Internal").ap()
        tap_scale = nc.dram_tensor("tap_scale", [HEADS + QUAD, 1], F32, kind="Internal").ap()

        w_gu = sb("w_gu", [P, 2, LB, 2 * INNER], F16)
        w_dn = sb("w_dn", [P, 2, IC, L], F16)
        ident = sb("ident", [P, P], F32)
        ident16 = sb("ident16", [P, 2, P], F16)
        x_in = sb("x_in", [P, 4, L], F32)
        c_in = sb("c_in", [P, 2, L], F32)
        t_in = sb("t_in", [P, 2, 2, L], F16)
        c_scaled = sb("c_scaled", [P, L], F32)
        q_rows = sb("q_rows", [P, L], F32)
        c_cols = sb("c_cols", [P, LB * 2, EXT], F32)
        q_cols = sb("q_cols", [P, 2, LB * 2, EXT], F32)
        pair32 = sb("pair32", [P, LB * 2, PAIRS], F32)
        pair_hi = sb("pair_hi", [P, 2, LB * 2, PAIRS], F16)
        pair_lo = sb("pair_lo", [P, 2, LB * 2, PAIRS], F16)
        z = sb("z", [P, 2, 8, ZW], F32)
        z1 = sb("z1", [P, 2, 4, HALF], F32)
        z2 = sb("z2", [P, 2, 2, HALF], F32)
        z_wrap = sb("z_wrap", [P, 2, 24], F32)
        o_cols = sb("o_cols", [P, 2, LB, P], F32)
        bn = sb("bn", [P, 2, 6], F32)
        head_small = sb("head_small", [P, 4, 17], F32)
        tap_factor = sb("tap_factor", [P, 2, QUAD], F32)
        x1 = sb("x1", [P, 2, QUAD, L], F32)
        xn_rows = sb("xn_rows", [P, L], F32)
        xn_cols = sb("xn_cols", [P, 2, 2, LB, ROWS], F16)
        silu_g = sb("silu_g", [P, 2, ROWS], F32)
        h32 = sb("h32", [P, 2, ROWS], F32)
        h = sb("h", [P, 2, IC, ROWS], F16)
        square = sb("square", [P, 2, L], F32)
        tile_small = sb("tile_small", [P, 2, 4], F32)
        const = sb("const", [P, 24], F32)
        k_small = sb("k_small", [HEADS, 8], F32)
        scales = sb("scales", [P, (GU + IC) * LB], F16)
        scale_parts = sb("scale_parts", [P, 4, (GU + IC) * LB], F32)
        kp = silu_g[0:HEADS].rearrange("p a s -> p (a s)")[:, 0:P + L]
        kp_split = h32[0:HEADS].rearrange("p a s -> p (a s)")[:, 0:P + L].bitcast(F16).rearrange(
            "p (a s) -> p a s", a=2)
        packed_gu = x1[:, 1].rearrange("p q l -> p (q l)").bitcast(I32)[:, 0:GU * LB * WORDS]
        packed_dn = square[:, :, :].rearrange("p a l -> p (a l)").bitcast(I32)[:, 0:LB * IC * WORDS]
        VW = 6 * LB * WORDS
        h_words = h[:, :, :, :].rearrange("p a c s -> p (a c s)").bitcast(I32)
        unpacked = [h_words[:, n * 4 * VW:(n + 1) * 4 * VW] for n in range(3)]
        DW = 2 * LB * P // 2
        g_words = silu_g[:, :, :].rearrange("p a s -> p (a s)").bitcast(I32)
        diag = [words[:, at:at + DW].bitcast(F16).rearrange("p (s j o) -> p s j o", s=2, j=LB)
                for words, at in ((h_words, 12 * VW), (h_words, 12 * VW + DW), (g_words, 0), (g_words, DW))]
        x_words = xn_cols[:, 1].rearrange("p a c s -> p (a c s)").bitcast(I32)
        signs = [x_words[:, n * VW:(n + 1) * VW] for n in range(2)]
        sizes = [x_words[:, (n + 2) * VW:(n + 3) * VW] for n in range(2)]

        PEAK, CPOW, CREC, MEAN, VAR, VE, RS, QS, QB, RF, MEAN2, VAR2, VE2, RS2, QB2, NEG, NEG2 = range(17)
        (MINUS_HALF, TANH_X, TANH_F, MAX_W, MAX_D, PEAK_W, PEAK_D, POW_W, POW_D, REC_W, REC_D, NORM_W, NORM_D,
         GATE_S, H_S, INV, INV2, EPS3) = range(18)

        def col(n):
            return const[:, n:n + 1]

        pair_bank = [[ps("gate0", [P, ROWS]), ps("up0", [P, ROWS])], [ps("gate1", [P, ROWS]), ps("up1", [P, ROWS])]]
        y_bank = pair_bank[1]
        conv_bank = ps("conv", [P, 2, 512])
        turn_a = ps("turn_a", [P, 512])
        turn_b = ps("turn_b", [P, 512])

        small_in, k_loaded, gu_loaded, dn_loaded, scales_in = sem("small_in"), sem("k_loaded"), sem("gu_loaded"), sem("dn_loaded"), sem("scales_in")
        x_loaded = [sem(f"x_loaded{n}") for n in range(4)]
        c_loaded = [sem(f"c_loaded{n}") for n in range(2)]
        t_loaded = [sem(f"t_loaded{n}") for n in range(2)]
        factor_loaded = [sem(f"factor_loaded{n}") for n in range(2)]
        taps_stored, factors_stored, ident_in = sem("taps_stored"), sem("factors_stored"), sem("ident_in")
        stored = [sem(f"stored{n}") for n in range(2)]
        z_zeroed = sem("z_zeroed")
        zeroed, k_step, w_small, w_peak, tanh_done, ident_cast = (
            sem("zeroed"), sem("k_step"), sem("w_small"), sem("w_peak"), sem("tanh_done"), sem("ident_cast"))
        bits_done, unpack_done, diagonals_made, w_turned, w_taken, scales_split = (
            sem("bits_done"), sem("unpack_done"), sem("diagonals_made"), sem("w_turned"), sem("w_taken"),
            sem("scales_split"))
        c_peak, x_moments, c_clamped, x_aggr, c_pow, var_ready, c_recip = (
            sem("c_peak"), sem("x_moments"), sem("c_clamped"), sem("x_aggr"), sem("c_pow"), sem("var_ready"),
            sem("c_recip"))
        rs_ready, q_scale, q_affine, row_factor = sem("rs_ready"), sem("q_scale"), sem("q_affine"), sem("row_factor")
        c_rows_ready, q_rows_ready, c_turned, q_turned = (
            sem("c_rows_ready"), sem("q_rows_ready"), sem("c_turned"), sem("q_turned"))
        c_cols_ready, q_cols_ready, pairs_ready, pairs_hi, pairs_lo = (
            sem("c_cols_ready"), sem("q_cols_ready"), sem("pairs_ready"), sem("pairs_hi"), sem("pairs_lo"))
        conv_done, z_filled, z1_done, z2_done, wrap_done, o_summed, o_ready = (
            sem("conv_done"), sem("z_filled"), sem("z1_done"), sem("z2_done"), sem("wrap_done"), sem("o_summed"),
            sem("o_ready"))
        out_turned, x1_ready, x1_moments, x1_aggr, var2_ready, rs2_ready, xn_affine = (
            sem("out_turned"), sem("x1_ready"), sem("x1_moments"), sem("x1_aggr"), sem("var2_ready"),
            sem("rs2_ready"), sem("xn_affine"))
        xn_rows_ready, xn_turned, xn_hi, xn_lo = (
            sem("xn_rows_ready"), sem("xn_turned"), sem("xn_hi"), sem("xn_lo"))
        gate_done, up_done, silu_done, h_ready, h_hi, h_lo = (
            sem("gate_done"), sem("up_done"), sem("silu_done"), sem("h_ready"), sem("h_hi"), sem("h_lo"))
        y_done, squared, mean_square, y_rs, y_scale, out_ready = (
            sem("y_done"), sem("squared"), sem("mean_square"), sem("y_rs"), sem("y_scale"), sem("out_ready"))

        def small(q, c, n=1):
            return head_small[:, q % 4, c:c + n]

        def spread(ap, step, count):
            a = [list(pair) for pair in ap.ap]
            return bass.AP(tensor=ap.tensor, offset=ap.offset, ap=[a[0], a[1], [step, count], a[2]])

        def pairs(eng, grp, q, n):
            if n == 0:
                wait(eng, pairs_hi, grp.head(q) * 2)
                wait(eng, pairs_lo, grp.head(q) * 2)
                eng.wait_ge(c_cols_ready, grp.head(q) * 2 + 2)
            g = slice(4 * n, 4 * n + 4)
            first = c_cols[:, g, 0:HALF]
            eng.tensor_tensor(pair32[:, g, 0:4 * HALF].rearrange("p g (d c) -> p g d c", d=4),
                              spread(first, 0, 4), spread(first, 8, 4), ALU.mult).then_inc(pairs_ready, 1)
            eng.tensor_tensor(pair32[:, g, 4 * HALF:PAIRS], c_cols[:, g, 0:32], c_cols[:, g, 32:64],
                              ALU.mult).then_inc(pairs_ready, 1)

        def pairs_low(eng, grp, q, n):
            eng.wait_ge(pairs_hi, grp.head(q) * 2 + n + 1)
            g = slice(4 * n, 4 * n + 4)
            eng.tensor_tensor(pair_lo[:, q % 2, g, :], pair32[:, g, :], pair_hi[:, q % 2, g, :],
                              ALU.subtract).then_inc(pairs_lo, 1)

        def diagonals(eng, w, part):
            _, is_down, tile, c0, count = PIECES[w]
            c = GU * LB + tile * IC + c0 if is_down else tile * LB
            one, factor = ident16[:, is_down, :], scale_parts[:, part, c:c + count]
            return eng.tensor_tensor(diag[w % 4][:, part, 0:count, :],
                                     bass.AP(tensor=one.tensor, offset=one.offset,
                                             ap=[list(one.ap[0]), [0, count], list(one.ap[1])]),
                                     bass.AP(tensor=factor.tensor, offset=factor.offset,
                                             ap=[list(factor.ap[0]), list(factor.ap[1]), [0, P]]), ALU.mult)

        PAIRED = (GROUPS - 3) // 2

        def run_groups(eng, group_program):
            group_program(static_group(0))
            group_program(static_group(1))
            with eng.Fori(0, PAIRED) as turn:
                group_program(Group(turn * 2 + 2, turn + 1, 0))
                group_program(Group(turn * 2 + 3, turn + 1, 1))
            group_program(static_group(GROUPS - 1))
            group_program(static_group(GROUPS))

        def feeds(grp):
            return grp.prev().tiles() if not isinstance(grp.n, int) or grp.n > 0 else []

        def feed_units(grp):
            late = 3 * (QUAD - len(feeds(grp)))
            return [(t, t - late) for t in range(UNITS + 2)]

        block = es.enter_context(nc.Block())

        @block.sync
        def _(sp):
            def rows_of(tensor, grp, q, half):
                if isinstance(grp.n, int):
                    channels = slice(grp.head(q) * HD, grp.head(q) * HD + HD)
                else:
                    channels = bass.ds(grp.n * (QUAD * HD) + (q - LEAD) * HD, HD)
                return tensor[8 * half:8 * half + 8, channels, :].rearrange("b i l -> i b l")

            def load_c(grp, q):
                wait(sp, c_rows_ready, grp.head(q) - 1)
                for half in range(2):
                    sp.dma_start(c_in[64 * half:64 * half + 64, q % 2, :],
                                 rows_of(ctx, grp, q, half)).then_inc(c_loaded[q % 2], 16)

            def load_x(grp, q):
                wait(sp, x1_ready, grp.head(q) - 3)
                for half in range(2):
                    sp.dma_start(x_in[64 * half:64 * half + 64, q % 4, :],
                                 rows_of(x, grp, q, half)).then_inc(x_loaded[q % 4], 16)

            def load_taps(grp, q):
                wait(sp, conv_done, grp.head(q) * LB - LB)
                if isinstance(grp.n, int):
                    first = toeplitz[grp.head(q):grp.head(q) + 1, 0, 1:1 + L]
                else:
                    first = toeplitz[bass.ds(grp.head(q), 1), 0, 1:1 + L]
                windows = bass.AP(tensor=first.tensor, offset=first.offset, ap=[[1, P], [P + L, 2], [1, L]])
                sp.dma_start(t_in[:, q % 2, :, :], windows).then_inc(t_loaded[q % 2], 16)

            def load_factor(grp):
                skipped = grp.tiles()[0]
                if isinstance(grp.n, int):
                    first = tap_scale[grp.head(skipped):grp.head(QUAD), 0:1]
                else:
                    first = tap_scale[bass.ds(grp.head(0), QUAD), 0:1]
                everywhere = bass.AP(tensor=first.tensor, offset=first.offset, ap=[[0, P], [1, QUAD - skipped]])
                sp.dma_start(tap_factor[:, grp.parity, skipped:], everywhere).then_inc(factor_loaded[grp.parity], 16)

            def store(grp, q):
                sp.wait_ge(out_ready, grp.head(q) + 1)
                for half in range(2):
                    sp.dma_start(rows_of(out, grp, q, half),
                                 x1[64 * half:64 * half + 64, grp.parity, q, :]).then_inc(stored[grp.parity], 16)

            def one_group(grp):
                tiles = feeds(grp)
                for t, u in feed_units(grp):
                    for stage, q, *_n in grp.stages(t):
                        if stage == "load_ct":
                            if grp.exists(q + 1):
                                load_taps(grp, q + 1)
                            if grp.exists(q + 2):
                                load_c(grp, q + 2)
                        elif stage == "load_x":
                            if grp.exists(q + 2):
                                load_x(grp, q + 2)
                            if q == 1 and grp.exists(QUAD):
                                load_factor(grp.next())
                    if u >= 26 and (u - 26) % 3 == 0 and (u - 26) // 3 < len(tiles):
                        store(grp.prev(), tiles[(u - 26) // 3])

            first = static_group(0)
            sp.dma_start(scales[:, 0:GU * LB], gu_scales).then_inc(scales_in, 16)
            sp.dma_start(scales[:, GU * LB:], dn_scales).then_inc(scales_in, 16)
            sp.dma_start(ident[:, :], identity).then_inc(ident_in, 16)
            sp.dma_start(packed_gu, gu_packed).then_inc(gu_loaded, 16)
            load_c(first, LEAD)
            load_x(first, LEAD)
            sp.dma_start(const[:, TANH_X:TANH_X + 1], g_xattn.partition_broadcast(P)).then_inc(small_in, 16)
            sp.dma_start(const[:, TANH_F:TANH_F + 1], g_ffn.partition_broadcast(P)).then_inc(small_in, 16)
            sp.wait_ge(zeroed, 1)
            sp.dma_start(kp[:, P:], taps).then_inc(k_loaded, 16)
            sp.dma_start(k_small[:, 0:1], skip).then_inc(k_loaded, 16)
            sp.dma_start(packed_dn, dn_packed).then_inc(dn_loaded, 16)
            sp.wait_ge(k_step, 8)
            sp.dma_start(toeplitz, kp_split[:, :, :]).then_inc(taps_stored, 16)
            sp.wait_ge(taps_stored, 16)
            load_taps(first, LEAD)
            load_c(first, LEAD + 1)
            load_x(first, LEAD + 1)
            sp.wait_ge(k_step, 9)
            sp.dma_start(tap_scale[0:HEADS], k_small[:, 3:4]).then_inc(factors_stored, 16)
            sp.dma_start(tap_scale[HEADS:], k_small[0:QUAD, 3:4]).then_inc(factors_stored, 16)
            sp.wait_ge(factors_stored, 32)
            load_factor(first)
            load_factor(first.next())
            run_groups(sp, one_group)
            for n in range(2):
                sp.wait_ge(stored[n], 2 * 16 * HEADS // 2)

        @block.tensor
        def _(pe):
            def turn(bank, src, done):
                for b in range(LB):
                    mm = pe.transpose(bank[:, P * b:P * b + P], src[:, b], ident[:, :])
                mm.then_inc(done, 1)

            def turned_out_before(grp, q):
                return grp.head(q) - (1 if q == 1 else 2)

            def turned_in_before(grp, q):
                heads = grp.head(q + (3 if q < QUAD - 1 else 2))
                return min(heads, HEADS) if isinstance(heads, int) else heads

            def turn_c(grp, q):
                wait(pe, c_cols_ready, grp.head(q) * 2)
                wait(pe, x1_ready, turned_out_before(grp, q))
                pe.wait_ge(c_rows_ready, grp.head(q) + 1)
                turn(turn_a, c_scaled[:, :].rearrange("p (b t) -> p b t", b=LB), c_turned)

            def turn_q(grp, q):
                wait(pe, q_cols_ready, grp.head(q) * 2)
                wait(pe, xn_lo, turned_out_before(grp, q))
                pe.wait_ge(q_rows_ready, grp.head(q) + 1)
                turn(turn_b, q_rows[:, :].rearrange("p (b t) -> p b t", b=LB), q_turned)

            def turn_out(grp, q):
                pe.wait_ge(c_cols_ready, turned_in_before(grp, q) * 2)
                wait(pe, x1_ready, grp.head(q))
                pe.wait_ge(o_ready, (grp.head(q) + 1) * LB)
                turn(turn_a, o_cols[:, q % 2], out_turned)

            def turn_x(grp, q):
                pe.wait_ge(q_cols_ready, turned_in_before(grp, q) * 2)
                wait(pe, xn_lo, grp.head(q))
                pe.wait_ge(xn_rows_ready, grp.head(q) + 1)
                turn(turn_b, xn_rows[:, :].rearrange("p (b t) -> p b t", b=LB), xn_turned)

            def conv(grp, q, n):
                wait(pe, z_filled, (grp.head(q) * LB + n) * 3)
                if n == 0:
                    pe.wait_ge(t_loaded[q % 2], (grp.uses(q, 2) + 1) * 16)
                if n % 2 == 0:
                    pe.wait_ge(pairs_lo, grp.head(q) * 2 + n // 2 + 1)
                for b in range(n + 1):
                    for part, moving in ((0, (pair_hi, pair_lo)), (1, (pair_hi,))):
                        w = t_in[:, q % 2, part, (n - b) * P:(n - b + 1) * P]
                        for m in moving:
                            for half in range(2):
                                mm = pe.matmul(conv_bank[:, half, 0:PAIRS], w, m[:, q % 2, 2 * b + half, :],
                                               start=(b == 0 and part == 0 and m is pair_hi),
                                               stop=(b == n and part == 1))
                mm.then_inc(conv_done, 1)

            def products(bank, steps):
                for k, (sta, mov) in enumerate(steps):
                    pe.matmul(bank, sta(0), mov(0), start=(k == 0), stop=False)
                    pe.matmul(bank, sta(0), mov(1), start=False, stop=False)
                    mm = pe.matmul(bank, sta(1), mov(0), start=False, stop=(k == len(steps) - 1))
                return mm

            def gate_or_up(grp, u, up):
                f = grp.n * IC
                tiles = grp.tiles()
                if u == 0 and not up:
                    if isinstance(grp.n, int) and grp.n == 0:
                        pe.wait_ge(w_taken, 2 * len(PIECES))
                    pe.wait_ge(xn_lo, grp.head(tiles[-1]) + 1)
                if u == 1:
                    wait(pe, out_ready, grp.head(tiles[0]))
                elif u > 1 and up:
                    pe.wait_ge(h_ready, f + u - 1)
                elif u > 1:
                    pe.wait_ge(silu_done, f + u - 1)
                o = (IC * up + u) * P
                steps = [(lambda part, b=b: w_gu[:, part, b, o:o + P],
                          lambda part, b=b: xn_cols[:, grp.parity, part, b, grp.columns()]) for b in range(LB)]
                products(pair_bank[u % 2][up][:, grp.columns()], steps).then_inc(up_done if up else gate_done, 1)

            def down(grp, s, part):
                f = grp.n * IC
                place = grp.tiles().index(s)
                if part == 0:
                    if place == 0:
                        pe.wait_ge(silu_done, f + IC - 1)
                    elif place == 1:
                        pe.wait_ge(h_ready, f + IC - 1)
                    else:
                        pe.wait_ge(out_ready, grp.head(s) - 1)
                for c in DOWN_PARTS[part]:
                    if place == 0:
                        pe.wait_ge(h_lo, f + c + 1)
                    bank = y_bank[place % 2][:, :]
                    rows = slice(s * P, s * P + P)
                    pe.matmul(bank, h[:, 0, c, rows], w_dn[:, 0, c, :], start=(c == 0), stop=False)
                    pe.matmul(bank, h[:, 0, c, rows], w_dn[:, 1, c, :], start=False, stop=False)
                    mm = pe.matmul(bank, h[:, 1, c, rows], w_dn[:, 0, c, :], start=False, stop=(c == IC - 1))
                if part == 2:
                    mm.then_inc(y_done, 1)

            def weights(w):
                batch, is_down, tile, c0, count = PIECES[w]
                if w >= 2:
                    pe.wait_ge(w_taken, 2 * (w - 1))
                pe.wait_ge(unpack_done, batch + 1)
                values = unpacked[batch % 3].bitcast(F16)
                for part in range(2):
                    pe.wait_ge(diagonals_made, 2 * w + part + 1)
                    for j in range(count):
                        c = (tile - BATCHES[batch][1]) * (IC if is_down else LB) + c0 + j
                        mm = pe.matmul(pair_bank[w % 2][part][:, P * j:P * j + P], values[:, P * c:P * c + P],
                                       diag[w % 4][:, part, j, :], start=True, stop=True)
                    mm.then_inc(w_turned, 1)

            def one_group(grp):
                tiles = feeds(grp)
                for t, u in feed_units(grp):
                    for stage, q, *n in grp.stages(t):
                        if stage == "conv":
                            conv(grp, q, n[0])
                        elif stage == "turn_c":
                            turn_c(grp, q)
                        elif stage == "turn_q":
                            turn_q(grp, q)
                        elif stage == "turn_out":
                            turn_out(grp, q)
                        elif stage == "turn_x":
                            turn_x(grp, q)
                    if tiles and 0 <= u < 2 * IC:
                        gate_or_up(grp.prev(), u // 2, u % 2)
                    elif tiles and u >= 0 and (u - 2 * IC) // 3 < len(tiles):
                        down(grp.prev(), tiles[(u - 2 * IC) // 3], (u - 2 * IC) % 3)
                    elif not tiles:
                        for w in pieces_at(t):
                            weights(w)

            pe.wait_ge(ident_in, 16)
            run_groups(pe, one_group)

        @block.scalar
        def _(act):
            def scale_c(grp, q):
                wait(act, c_turned, grp.head(q))
                act.wait_ge(c_recip, grp.head(q) + 1)
                act.activation(c_scaled[:, :].rearrange("p (b t) -> p b t", b=LB)[:, :, ::-1],
                               c_in[:, q % 2, :].rearrange("p (b t) -> p b t", b=LB),
                               ACT.Copy, scale=small(q, CREC)).then_inc(c_rows_ready, 1)

            def make_q(grp, q):
                wait(act, q_turned, grp.head(q))
                act.wait_ge(q_affine, grp.head(q) + 1)
                act.activation(q_rows[:, :], x_in[:, q % 4, :], ACT.Identity, scale=small(q, QS),
                               bias=small(q, QB)).then_inc(q_rows_ready, 1)

            def extend(dst, bank, done, scale):
                src = bank[:, :].rearrange("p (g c) -> p g c", c=HALF)
                act.activation(dst[:, :, 0:HALF], src, ACT.Copy, scale=scale).then_inc(done, 1)
                act.activation(dst[:, :, HALF:EXT], src[:, :, 0:EXT - HALF], ACT.Copy, scale=scale).then_inc(done, 1)

            def take_c(grp, q):
                wait(act, pairs_ready, grp.head(q) * 4)
                act.wait_ge(c_turned, grp.head(q) + 1)
                extend(c_cols, turn_a, c_cols_ready, 32.0)

            def take_q(grp, q):
                wait(act, z_filled, (grp.head(q) - 1) * LB * 3)
                act.wait_ge(q_turned, grp.head(q) + 1)
                extend(q_cols[:, q % 2], turn_b, q_cols_ready, 1.0)

            def pairs_high(grp, q, n):
                if n == 0:
                    wait(act, conv_done, (grp.head(q) - 1) * LB)
                act.wait_ge(pairs_ready, grp.head(q) * 4 + 2 * n + 2)
                act.activation(pair_hi[:, q % 2, 4 * n:4 * n + 4, :], pair32[:, 4 * n:4 * n + 4, :],
                               ACT.Copy).then_inc(pairs_hi, 1)

            def normalise(grp, q):
                wait(act, xn_turned, grp.head(q))
                act.wait_ge(xn_affine, grp.head(q) + 1)
                act.activation(xn_rows[:, :].rearrange("p (b k m) -> p b m k", b=LB, k=4),
                               x1[:, grp.parity, q, :].rearrange("p (b m k) -> p b m k", b=LB, k=4),
                               ACT.Identity, scale=small(q, RS2),
                               bias=small(q, QB2)).then_inc(xn_rows_ready, 1)

            def x_high(grp, q):
                act.wait_ge(xn_turned, grp.head(q) + 1)
                act.activation(xn_cols[:, grp.parity, 0, :, q * P:q * P + P],
                               turn_b[:, :].rearrange("p (b r) -> p b r", b=LB), ACT.Copy).then_inc(xn_hi, 1)

            def silu(grp, u):
                f = grp.n * IC
                if u >= 2:
                    act.wait_ge(h_ready, f + u - 1)
                act.wait_ge(gate_done, f + u + 1)
                act.activation(silu_g[:, u % 2, grp.columns()], pair_bank[u % 2][0][:, grp.columns()], ACT.Silu,
                               scale=col(GATE_S)).then_inc(silu_done, 1)

            def h_high(grp, u):
                f = grp.n * IC
                act.wait_ge(h_ready, f + u + 1)
                act.activation(h[:, 0, u, grp.columns()], h32[:, u % 2, grp.columns()], ACT.Copy).then_inc(h_hi, 1)

            def take_weights(w):
                _, is_down, tile, c0, count = PIECES[w]
                if w == 0:
                    act.wait_ge(w_small, 10)
                cols = slice(tile * P, tile * P + P)
                for part in range(2):
                    act.wait_ge(w_turned, 2 * w + part + 1)
                    dst = w_dn[:, part, c0:c0 + count, cols] if is_down else w_gu[:, part, :, cols]
                    act.activation(dst, pair_bank[w % 2][part][:, 0:count * P].rearrange("p (c o) -> p c o", o=P),
                                   ACT.Copy, scale=col(NORM_D if is_down else NORM_W)).then_inc(w_taken, 1)

            def square_y(grp, s):
                if grp.tiles().index(s) >= 2:
                    act.wait_ge(mean_square, grp.head(s) - 1)
                act.wait_ge(y_done, grp.head(s) + 1)
                act.activation(square[:, s % 2, :], y_bank[grp.tiles().index(s) % 2][:, :], ACT.Square,
                               scale=L ** -0.5, accum_out=tile_small[:, s % 2, 0:1]).then_inc(squared, 2)

            def one_group(grp):
                tiles = feeds(grp)
                for t, u in feed_units(grp):
                    if tiles:
                        if u % 2 == 1 and 0 <= u < 2 * IC:
                            silu(grp.prev(), u // 2)
                        if u % 2 == 0 and 2 <= u <= 2 * IC:
                            h_high(grp.prev(), u // 2 - 1)
                        if u >= 25 and (u - 25) % 3 == 0 and (u - 25) // 3 < len(tiles):
                            square_y(grp.prev(), tiles[(u - 25) // 3])
                    for stage, q, *n in grp.stages(t):
                        if stage == "turn_c":
                            take_c(grp, q)
                        elif stage == "turn_q":
                            take_q(grp, q)
                        elif stage == "turn_x":
                            x_high(grp, q)
                    for w in pieces_at(t) if not tiles else ():
                        take_weights(w)
                    for stage, q, *n in grp.stages(t):
                        if stage == "pairs":
                            pairs_high(grp, q, n[0])
                        elif stage == "turn_out":
                            normalise(grp, q)
                        elif stage == "stats":
                            scale_c(grp, q)
                            make_q(grp, q)

            act.wait_ge(small_in, 32)
            act.activation(col(TANH_X), col(TANH_X), ACT.Tanh).then_inc(tanh_done, 1)
            act.activation(col(TANH_F), col(TANH_F), ACT.Tanh).then_inc(tanh_done, 1)
            first = static_group(0)
            scale_c(first, LEAD)
            make_q(first, LEAD)
            run_groups(act, one_group)

        @block.gpsimd
        def _(pool):
            def q_scalars(grp, q):
                n = grp.head(q)
                pool.wait_ge(var_ready, 2 * n + 2)
                pool.tensor_tensor(small(q, RS), small(q, VE), col(MINUS_HALF), ALU.pow).then_inc(rs_ready, 1)
                pool.wait_ge(c_recip, n + 1)
                pool.wait_ge(rs_ready, n + 1)
                pool.tensor_tensor(small(q, QS), small(q, RS), small(q, CPOW), ALU.mult).then_inc(q_scale, 1)
                pool.wait_ge(q_scale, n + 1)
                pool.tensor_tensor(small(q, QB), small(q, NEG), small(q, QS), ALU.mult).then_inc(q_affine, 1)

            def attention_factor(grp, q):
                n = grp.head(q)
                if q == QUAD or isinstance(n, int) and n == 0:
                    home = grp.next() if q == QUAD else grp
                    pool.wait_ge(factor_loaded[home.parity], (home.halved + 1) * 16)
                pool.wait_ge(c_recip, n + 1)
                parity = grp.parity if q < QUAD else 1 - grp.parity
                pool.tensor_tensor(small(q, RF), small(q, CPOW), tap_factor[:, parity, q % 4:q % 4 + 1],
                                   ALU.mult).then_inc(row_factor, 1)

            def norm_scalars(grp, q):
                n = grp.head(q)
                pool.wait_ge(var2_ready, 2 * n + 2)
                pool.tensor_tensor(small(q, RS2), small(q, VE2), col(MINUS_HALF), ALU.pow).then_inc(rs2_ready, 1)
                pool.wait_ge(rs2_ready, n + 1)
                pool.tensor_tensor(small(q, QB2), small(q, NEG2), small(q, RS2), ALU.mult).then_inc(xn_affine, 1)

            def y_scalars(grp, s):
                n = grp.head(s)
                pool.wait_ge(squared, 2 * n + 2)
                pool.tensor_tensor(tile_small[:, s % 2, 1:2], tile_small[:, s % 2, 0:1], col(EPS3),
                                   ALU.add).then_inc(mean_square, 1)
                pool.wait_ge(mean_square, n + 1)
                pool.tensor_tensor(tile_small[:, s % 2, 2:3], tile_small[:, s % 2, 1:2], col(MINUS_HALF),
                                   ALU.pow).then_inc(y_rs, 1)
                if grp.tiles().index(s) >= 2:
                    pool.wait_ge(out_ready, n - 1)
                pool.wait_ge(y_rs, n + 1)
                pool.tensor_tensor(tile_small[:, s % 2, 3:4], tile_small[:, s % 2, 2:3], col(TANH_F),
                                   ALU.mult).then_inc(y_scale, 1)

            def one_group(grp):
                tiles = feeds(grp)
                for t, u in feed_units(grp):
                    if u >= 25 and (u - 25) % 3 == 0 and (u - 25) // 3 < len(tiles):
                        y_scalars(grp.prev(), tiles[(u - 25) // 3])
                    for w in pieces_at(t) if not tiles else ():
                        if w >= 4:
                            pool.wait_ge(w_turned, 2 * (w - 3))
                        if w == 2:
                            pool.wait_ge(k_step, 8)
                        diagonals(pool, w, 0).then_inc(diagonals_made, 1)
                        diagonals(pool, w, 1).then_inc(diagonals_made, 1)
                    for stage, q, *n in grp.stages(t):
                        if stage == "stats":
                            q_scalars(grp, q)
                            if not tiles and q == LEAD + 1:
                                attention_factor(grp, LEAD)
                            attention_factor(grp, q)
                        elif stage == "pairs" and tiles:
                            pairs(pool, grp, q, n[0])
                        elif stage == "conv" and tiles and n[0] == 2 and grp.exists(q + 1):
                            pairs_low(pool, grp, q + 1, 0)
                            pairs_low(pool, grp, q + 1, 1)
                        elif stage == "turn_out":
                            norm_scalars(grp, q)

            pool.memset(z[:, :, :, :], 0.0).then_inc(z_zeroed, 1)
            pool.wait_ge(w_small, 2)
            pool.partition_all_reduce(col(PEAK_W), col(MAX_W), P, RMAX).then_inc(w_peak, 1)
            pool.partition_all_reduce(col(PEAK_D), col(MAX_D), P, RMAX).then_inc(w_peak, 1)
            first = static_group(0)
            q_scalars(first, LEAD)
            pool.wait_ge(ident_cast, 2)
            pool.wait_ge(scales_split, 4)
            run_groups(pool, one_group)

        @block.vector
        def _(dve):
            def stats(grp, q):
                n = grp.head(q)
                dve.wait_ge(c_loaded[q % 2], (grp.uses(q, 2) + 1) * 32)
                dve.tensor_reduce(small(q, PEAK), c_in[:, q % 2, :], AX_X, ALU.max,
                                  apply_absolute_value=True).then_inc(c_peak, 1)
                dve.wait_ge(x_loaded[q % 4], (grp.uses(q, 4) + 1) * 32)
                dve.bn_stats(bn[:, 0, :], x_in[:, q % 4, :]).then_inc(x_moments, 1)
                dve.wait_ge(x_moments, n + 1)
                dve.wait_ge(c_peak, n + 1)
                dve.tensor_scalar(small(q, PEAK), small(q, PEAK), 2.0 ** -60, None, ALU.max).then_inc(c_clamped, 1)
                dve.bn_aggr(small(q, MEAN, 2), bn[:, 0, :]).then_inc(x_aggr, 1)
                dve.wait_ge(c_clamped, n + 1)
                dve.tensor_scalar(small(q, CPOW).bitcast(I32), small(q, PEAK).bitcast(I32), 0x7F800000, None,
                                  ALU.bitwise_and).then_inc(c_pow, 1)
                dve.wait_ge(x_aggr, n + 1)
                dve.tensor_scalar(small(q, NEG), small(q, MEAN), -1.0, None, ALU.mult).then_inc(var_ready, 1)
                dve.tensor_scalar(small(q, VE), small(q, VAR), LN_EPS, 1024.0, ALU.add, ALU.mult).then_inc(var_ready, 1)
                dve.wait_ge(c_pow, n + 1)
                dve.reciprocal(small(q, CREC), small(q, CPOW)).then_inc(c_recip, 1)

            def weigh(grp, q, n):
                m = grp.head(q) * LB + n
                if n == 0:
                    dve.wait_ge(q_cols_ready, grp.head(q) * 2 + 2)
                    wait(dve, out_turned, grp.head(q) - 1)
                wait(dve, z1_done, m)
                wait(dve, wrap_done, m)
                dve.wait_ge(conv_done, m + 1)
                y = conv_bank[:, :, 0:HALF]
                ql = q_cols[:, q % 2, 2 * n:2 * n + 2, 0:HALF]
                dve.tensor_tensor(spread(z[:, :, 0, 0:HALF], ZW + 8, 4), spread(y, HALF, 4), spread(ql, 0, 4),
                                  ALU.mult).then_inc(z_filled, 1)
                dve.tensor_tensor(z[:, :, 4:7, 0:HALF], spread(conv_bank[:, :, HALF:2 * HALF], HALF, 3),
                                  spread(q_cols[:, q % 2, 2 * n:2 * n + 2, 8:8 + HALF], 8, 3),
                                  ALU.mult).then_inc(z_filled, 1)
                dve.tensor_tensor(z[:, :, 7, 0:HALF].rearrange("p g (k c) -> p g k c", k=2),
                                  spread(conv_bank[:, :, 4 * HALF:PAIRS], 0, 2),
                                  spread(q_cols[:, q % 2, 2 * n:2 * n + 2, 32:64], 32, 2),
                                  ALU.mult).then_inc(z_filled, 1)
                dve.wait_ge(z_filled, 3 * m + 3)
                wait(dve, z2_done, m)
                dve.tensor_tensor(z1[:, :, :, :], z[:, :, 0:4, 0:HALF], z[:, :, 4:8, 0:HALF],
                                  ALU.add).then_inc(z1_done, 1)
                wait(dve, o_ready, m)
                dve.tensor_reduce(z_wrap[:, :, :], z[:, :, 1:4, HALF:HALF + 24].rearrange("p g d c -> p g c d"), AX_X,
                                  ALU.add).then_inc(wrap_done, 1)
                dve.wait_ge(z1_done, m + 1)
                dve.tensor_tensor(z2[:, :, :, :], z1[:, :, 0:2, :], z1[:, :, 2:4, :], ALU.add).then_inc(z2_done, 1)
                dve.wait_ge(z2_done, m + 1)
                o = o_cols[:, q % 2, n, :].rearrange("p (g c) -> p g c", g=2)
                dve.tensor_tensor(o, z2[:, :, 0, :], z2[:, :, 1, :], ALU.add).then_inc(o_summed, 1)
                dve.wait_ge(wrap_done, m + 1)
                dve.wait_ge(o_summed, m + 1)
                dve.tensor_tensor(o[:, :, 0:24], o[:, :, 0:24], z_wrap[:, :, :], ALU.add).then_inc(o_ready, 1)

            def add_attention(grp, q):
                n = grp.head(q)
                if q == grp.tiles()[0]:
                    wait(dve, stored[grp.parity], (grp.halved * QUAD - LEAD * (1 - grp.parity)) * 2 * 16)
                dve.wait_ge(row_factor, n + 1)
                dve.wait_ge(out_turned, n + 1)
                dve.scalar_tensor_tensor(x1[:, grp.parity, q, :], turn_a[:, :], small(q, RF), x_in[:, q % 4, :],
                                         ALU.mult, ALU.add).then_inc(x1_ready, 1)
                dve.wait_ge(x1_ready, n + 1)
                dve.bn_stats(bn[:, 1, :], x1[:, grp.parity, q, :]).then_inc(x1_moments, 1)
                dve.wait_ge(x1_moments, n + 1)
                dve.tensor_copy(small(q, VE2), small(q, VE2))
                dve.bn_aggr(small(q, MEAN2, 2), bn[:, 1, :]).then_inc(x1_aggr, 1)
                dve.wait_ge(x1_aggr, n + 1)
                dve.tensor_scalar(small(q, NEG2), small(q, MEAN2), -1.0, None, ALU.mult).then_inc(var2_ready, 1)
                dve.tensor_scalar(small(q, VE2), small(q, VAR2), LN_EPS, 2.0 ** -16, ALU.add,
                                  ALU.mult).then_inc(var2_ready, 1)

            def x_low(grp, q):
                dve.wait_ge(xn_hi, grp.head(q) + 1)
                dve.tensor_tensor(xn_cols[:, grp.parity, 1, :, q * P:q * P + P],
                                  turn_b[:, :].rearrange("p (b r) -> p b r", b=LB),
                                  xn_cols[:, grp.parity, 0, :, q * P:q * P + P], ALU.subtract).then_inc(xn_lo, 1)

            def make_h(grp, u):
                f = grp.n * IC
                if u >= 2:
                    dve.wait_ge(h_hi, f + u - 1)
                dve.wait_ge(up_done, f + u + 1)
                dve.wait_ge(silu_done, f + u + 1)
                cols = grp.columns()
                dve.scalar_tensor_tensor(h32[:, u % 2, cols], pair_bank[u % 2][1][:, cols], col(H_S), silu_g[:, u % 2, cols],
                                         ALU.mult, ALU.mult).then_inc(h_ready, 1)

            def h_low(grp, u):
                dve.wait_ge(h_hi, grp.n * IC + u + 1)
                cols = grp.columns()
                dve.tensor_tensor(h[:, 1, u, cols], h32[:, u % 2, cols], h[:, 0, u, cols], ALU.subtract).then_inc(h_lo, 1)

            def finish(grp, s):
                dve.wait_ge(y_scale, grp.head(s) + 1)
                rows = x1[:, grp.parity, s, :]
                dve.scalar_tensor_tensor(rows, y_bank[grp.tiles().index(s) % 2][:, :], tile_small[:, s % 2, 3:4], rows, ALU.mult,
                                         ALU.add).then_inc(out_ready, 1)

            bits = [0]

            def unpack(batch):
                is_down, t0, nt = BATCHES[batch]
                per_tile = (IC if is_down else LB) * WORDS
                n = nt * per_tile
                if BATCHES[batch - 1][0] < is_down:
                    dve.wait_ge(dn_loaded, 16)
                words = (packed_dn if is_down else packed_gu)[:, t0 * per_tile:t0 * per_tile + n]
                if batch >= 3:
                    done = 1 + max(w for w, piece in enumerate(PIECES) if piece[0] == batch - 3)
                    dve.wait_ge(w_turned, 2 * done)
                nibbles = []
                for odd in range(2):
                    size, sign = sizes[odd][:, 0:n], signs[odd][:, 0:n]
                    if odd:
                        dve.tensor_scalar(size, words, 4, 0x07070707, ALU.logical_shift_right,
                                          ALU.bitwise_and).then_inc(bits_done, 1)
                        dve.tensor_scalar(sign, words, 1, 0x40404040, ALU.logical_shift_right,
                                          ALU.bitwise_and).then_inc(bits_done, 1)
                    else:
                        dve.tensor_scalar(size, words, 0x07070707, None, ALU.bitwise_and).then_inc(bits_done, 1)
                        dve.tensor_scalar(sign, words, 3, 0x40404040, ALU.logical_shift_left,
                                          ALU.bitwise_and).then_inc(bits_done, 1)
                    nibbles.append((size, sign))
                for odd, (size, sign) in enumerate(nibbles):
                    dve.wait_ge(bits_done, bits[0] + 2 * odd + 2)
                    dve.tensor_tensor(size, size, sign, ALU.bitwise_or).then_inc(bits_done, 1)
                bits[0] += 6
                for k in (0, 2, 1, 3):
                    dve.wait_ge(bits_done, bits[0] - 1 + k % 2)
                    values = unpacked[batch % 3][:, 0:4 * n].rearrange("p (c k j) -> p c k j", k=4, j=WORDS)[:, :, k, :]
                    dve.tensor_scalar(values, nibbles[k % 2][0].rearrange("p (c j) -> p c j", j=WORDS),
                                      9 if k < 2 else 1, -0x71FF7200, ALU.logical_shift_left,
                                      ALU.bitwise_and).then_inc(bits_done, 1)
                bits[0] += 4
                dve.wait_ge(bits_done, bits[0])
                dve.sem_inc(unpack_done, 1)

            def one_group(grp):
                tiles = feeds(grp)
                for t, u in feed_units(grp):
                    if tiles:
                        if u % 2 == 0 and 2 <= u <= 2 * IC:
                            make_h(grp.prev(), u // 2 - 1)
                        if u % 2 == 1 and 3 <= u <= 2 * IC + 1:
                            h_low(grp.prev(), (u - 3) // 2)
                        if u >= 26 and (u - 26) % 3 == 0 and (u - 26) // 3 < len(tiles):
                            finish(grp.prev(), tiles[(u - 26) // 3])
                    for w in pieces_at(t) if not tiles else ():
                        batch = PIECES[w][0]
                        if PIECES[w] == FIRST_PIECES[batch] and batch + 1 < len(BATCHES):
                            unpack(batch + 1)
                    for stage, q, *n in grp.stages(t):
                        if stage == "conv":
                            weigh(grp, q, n[0])
                        elif stage == "pairs" and not tiles:
                            pairs(dve, grp, q, n[0])
                        elif stage == "turn_out":
                            add_attention(grp, q)
                        elif stage == "turn_x":
                            x_low(grp, q)
                        elif stage == "stats":
                            if not tiles:
                                pairs_low(dve, grp, q - 1, 0)
                                pairs_low(dve, grp, q - 1, 1)
                            stats(grp, q)

            dve.memset(kp[:, 0:P], 0.0).then_inc(zeroed, 1)
            dve.memset(const[:, MINUS_HALF:MINUS_HALF + 1], -0.5).then_inc(zeroed, 1)
            dve.memset(head_small[:, :, :], 0.0).then_inc(zeroed, 1)
            dve.wait_ge(zeroed, 3)
            dve.wait_ge(scales_in, 32)
            dve.tensor_reduce(col(MAX_W), scales[:, 0:GU * LB], AX_X, ALU.max, apply_absolute_value=True).then_inc(w_small, 1)
            dve.tensor_reduce(col(MAX_D), scales[:, GU * LB:], AX_X, ALU.max, apply_absolute_value=True).then_inc(w_small, 1)
            dve.wait_ge(ident_in, 16)
            dve.tensor_copy(ident16[:, 1, :], ident[:, :]).then_inc(ident_cast, 1)
            dve.tensor_copy(ident16[:, 0, :].rearrange("p (k m) -> p k m", k=4),
                            ident[:, :].rearrange("p (m k) -> p k m", k=4)).then_inc(ident_cast, 1)
            rest, hi, lo, scaled = (scale_parts[:, c, :] for c in (3, 0, 1, 2))
            dve.tensor_scalar(scaled, scales[:, :], 2.0 ** 15 + 1, None, ALU.mult).then_inc(scales_split, 1)
            dve.wait_ge(scales_split, 1)
            dve.tensor_tensor(rest, scaled, scales[:, :], ALU.subtract).then_inc(scales_split, 1)
            dve.wait_ge(scales_split, 2)
            dve.tensor_tensor(hi, scaled, rest, ALU.subtract).then_inc(scales_split, 1)
            dve.wait_ge(scales_split, 3)
            dve.tensor_tensor(lo, scales[:, :], hi, ALU.subtract).then_inc(scales_split, 1)
            dve.wait_ge(scales_split, 4)
            dve.wait_ge(gu_loaded, 16)
            unpack(0)
            first = static_group(0)
            stats(first, LEAD)
            dve.wait_ge(k_loaded, 32)
            dve.tensor_tensor(kp[:, P:P + 1], kp[:, P:P + 1], k_small[:, 0:1], ALU.add).then_inc(k_step, 1)
            dve.wait_ge(k_step, 1)
            dve.tensor_reduce(k_small[:, 1:2], kp[:, P:], AX_X, ALU.max, apply_absolute_value=True).then_inc(k_step, 1)
            dve.wait_ge(k_step, 2)
            dve.tensor_scalar(k_small[:, 2:3], k_small[:, 1:2], 2.0 ** -60, None, ALU.max).then_inc(k_step, 1)
            dve.wait_ge(k_step, 3)
            dve.tensor_scalar(k_small[:, 4:5].bitcast(I32), k_small[:, 2:3].bitcast(I32), 0x7F800000, None,
                              ALU.bitwise_and).then_inc(k_step, 1)
            dve.wait_ge(k_step, 4)
            dve.reciprocal(k_small[:, 5:6], k_small[:, 4:5]).then_inc(k_step, 1)
            dve.wait_ge(k_step, 5)
            dve.tensor_scalar(kp[:, :], kp[:, :], k_small[:, 5:6], 32.0, ALU.mult, ALU.mult).then_inc(k_step, 1)
            dve.wait_ge(k_step, 6)
            dve.tensor_copy(kp_split[:, 0, :], kp[:, :]).then_inc(k_step, 1)
            dve.wait_ge(k_step, 7)
            dve.tensor_tensor(kp_split[:, 1, :], kp[:, :], kp_split[:, 0, :], ALU.subtract).then_inc(k_step, 1)
            dve.wait_ge(tanh_done, 2)
            dve.tensor_scalar(k_small[:, 3:4], k_small[:, 4:5], const[0:HEADS, TANH_X:TANH_X + 1], 2.0 ** -10, ALU.mult,
                              ALU.mult).then_inc(k_step, 1)

            dve.wait_ge(w_peak, 2)
            peaks, powers, recips = (const[:, c:c + 2] for c in (PEAK_W, POW_W, REC_W))
            dve.tensor_scalar(peaks, peaks, 2.0 ** -24, None, ALU.max).then_inc(w_small, 1)
            dve.wait_ge(w_small, 3)
            dve.tensor_scalar(powers.bitcast(I32), peaks.bitcast(I32), 0x7F800000, None,
                              ALU.bitwise_and).then_inc(w_small, 1)
            dve.wait_ge(w_small, 4)
            dve.reciprocal(recips, powers).then_inc(w_small, 1)
            dve.tensor_scalar(col(GATE_S), col(POW_W), 2.0 ** -8, None, ALU.mult).then_inc(w_small, 1)
            dve.wait_ge(w_small, 6)
            dve.tensor_scalar(const[:, NORM_W:NORM_W + 2], recips, 2.0 ** 14, None, ALU.mult).then_inc(w_small, 1)
            dve.tensor_scalar(col(H_S), col(REC_W), 2.0 ** -18, None, ALU.mult).then_inc(w_small, 1)
            dve.tensor_scalar(col(INV), col(REC_W), col(REC_W), col(REC_D), ALU.mult, ALU.mult).then_inc(w_small, 1)
            dve.wait_ge(w_small, 9)
            dve.tensor_scalar(col(INV2), col(INV), 2.0 ** -10, None, ALU.mult).then_inc(w_small, 1)
            dve.wait_ge(w_small, 10)
            dve.tensor_scalar(col(EPS3), col(INV2), col(INV2), RMS_EPS, ALU.mult, ALU.mult).then_inc(w_small, 1)
            dve.wait_ge(w_small, 11)

            dve.wait_ge(z_zeroed, 1)
            run_groups(dve, one_group)


def kernel(x, ctx_2048, g_xattn, g_ffn, L0_xattn_ssm_kernel, L0_xattn_D, L0_ffn_gate_up_packed, L0_ffn_gate_up_scales,
           L0_ffn_down_packed, L0_ffn_down_scales):
    import numpy as np
    import concourse.bacc as bacc
    from concourse.bass_utils import run_bass_kernel_spmd

    def packed_tiles(words):
        words = np.asarray(words)
        return np.ascontiguousarray(words.reshape(-1, P, words.shape[1]).transpose(1, 0, 2).reshape(P, -1))

    def scale_tiles(scales):
        scales = np.asarray(scales)
        return np.ascontiguousarray(scales.reshape(scales.shape[0], -1, P).transpose(2, 1, 0).reshape(P, -1))

    arrays = {
        "x": np.ascontiguousarray(x),
        "ctx": np.ascontiguousarray(ctx_2048),
        "g_xattn": np.ascontiguousarray(g_xattn),
        "g_ffn": np.ascontiguousarray(g_ffn),
        "taps": np.ascontiguousarray(L0_xattn_ssm_kernel),
        "skip": np.ascontiguousarray(L0_xattn_D).reshape(HEADS, 1),
        "gu_packed": packed_tiles(L0_ffn_gate_up_packed),
        "gu_scales": scale_tiles(L0_ffn_gate_up_scales),
        "dn_packed": packed_tiles(L0_ffn_down_packed),
        "dn_scales": scale_tiles(L0_ffn_down_scales),
        "identity": np.eye(P, dtype=np.float32),
    }
    nc = bacc.Bacc("TRN2", target_bir_lowering=False, num_devices=1)
    aps = [nc.dram_tensor(n, a.shape, mybir.dt.from_np(a.dtype), kind="ExternalInput").ap() for n, a in arrays.items()]
    out = nc.dram_tensor("out", (BATCH, CHANNELS, L), F32, kind="ExternalOutput").ap()
    flamingo_block(nc, *aps, out)
    result = run_bass_kernel_spmd(nc, [arrays], core_ids=[0])
    return result.results[0]["out"]
```
